# Optimizing a Trainium2 kernel written in Bass

```python
import numpy as np
import jax
import jax.numpy as jnp

def _softmax(x, axis=-1):
    return jax.nn.softmax(x, axis=axis)

def _gelu(x):
    return jax.nn.gelu(x, approximate=True)

def _silu(x):
    return jax.nn.silu(x)

def _sigmoid(x):
    return jax.nn.sigmoid(x)

def _layernorm(x, axis=-1, eps=1e-05):
    m = jnp.mean(x, axis=axis, keepdims=True)
    v = jnp.var(x, axis=axis, keepdims=True)
    return (x - m) / jnp.sqrt(v + eps)

def _scatter_add(tgt, idx, src, axis=0):
    return tgt.at[idx].add(src)

def _segment_sum(src, seg, n):
    return jax.ops.segment_sum(src, seg, n)
kernel_name = 'mk_prb_d1_jaxref_r4_ab9545'

def setup_inputs(seed: int=0):
    np.random.seed(seed)
    _w = jnp.asarray

    def _L0_attn_setup():
        import jax, jax.numpy as jnp
        import numpy as np
        D_MODEL = 512
        D_STATE = 64
        D_CONV = 4
        EXPAND = 2
        HEADDIM = 64
        NGROUPS = 1
        CHUNK = 64
        D_INNER = D_MODEL * EXPAND
        NHEADS = D_INNER // HEADDIM
        D_IN_PROJ = 2 * D_INNER + 2 * NGROUPS * D_STATE + NHEADS
        BATCH, SEQLEN = (2, 1024)
        RMS_EPS = 1e-06

        def elu_plus_one(x):
            return jax.nn.elu(x) + 1.0

        def softplus(x):
            return jnp.where(x > 20, x, jnp.log1p(jnp.exp(x)))

        def causal_conv1d(x, w, b):
            Bsz, L, Dn = x.shape
            k = w.shape[0]
            xp = jnp.transpose(jnp.pad(x, ((0, 0), (k - 1, 0), (0, 0))), (0, 2, 1))
            kern = jnp.transpose(w, (1, 0))[:, None, :]
            y = jax.lax.conv_general_dilated(xp, kern, (1,), 'VALID', feature_group_count=Dn, dimension_numbers=('NCH', 'OIH', 'NCH'))
            return jnp.transpose(y, (0, 2, 1)) + b

        def ssd_chunked(q, k, v, a, chunk_size):
            Bsz, H, L, N = q.shape
            S = chunk_size
            C = L // S
            qc = q.reshape(Bsz, H, C, S, N)
            kc = k.reshape(Bsz, H, C, S, N)
            vc = v.reshape(Bsz, H, C, S, -1)
            la = jnp.log(a).reshape(Bsz, H, C, S)
            cs = jnp.cumsum(la, axis=-1)
            causal = jnp.tril(jnp.ones((S, S), bool))
            logdec = jnp.where(causal, cs[..., :, None] - cs[..., None, :], -jnp.inf)
            att = jnp.einsum('bhcsn,bhctn->bhcst', qc, kc) * jnp.exp(logdec)
            y_intra = jnp.einsum('bhcst,bhctp->bhcsp', att, vc)
            total = cs[..., -1]
            k_scaled = kc * jnp.exp(total[..., None, None] - cs[..., None])
            states = jnp.einsum('bhcsn,bhcsp->bhcnp', k_scaled, vc)
            d_t = jnp.moveaxis(jnp.exp(total), 2, 0)
            s_t = jnp.moveaxis(states, 2, 0)

            def step(h, inp):
                d, s = inp
                return (d[..., None, None] * h + s, h)
            _, h_prev = jax.lax.scan(step, jnp.zeros_like(s_t[0]), (d_t, s_t))
            h_prev = jnp.moveaxis(h_prev, 0, 2)
            y_inter = jnp.einsum('bhcsn,bhcnp->bhcsp', qc * jnp.exp(cs)[..., None], h_prev)
            return (y_intra + y_inter).reshape(Bsz, H, L, -1)
        key = jax.random.key(seed)
        k0, k1, k2, k3 = jax.random.split(key, 4)
        u = jax.random.normal(k0, (BATCH, SEQLEN, D_MODEL), jnp.float32)
        in_proj_w = jax.random.normal(k1, (D_MODEL, D_IN_PROJ), jnp.float32) / np.sqrt(D_MODEL)
        conv_weight = jax.random.normal(k2, (D_CONV, D_INNER), jnp.float32) / np.sqrt(D_CONV)
        conv_bias = jnp.zeros((D_INNER,), jnp.float32)
        A_log = jnp.log(jnp.linspace(1.0, 16.0, NHEADS)).astype(jnp.float32)
        dt_init = jnp.exp(jnp.linspace(np.log(0.001), np.log(0.1), NHEADS))
        dt_bias = (dt_init + jnp.log(-jnp.expm1(-dt_init))).astype(jnp.float32)
        D_param = jnp.ones((NHEADS,), jnp.float32)
        norm_scale = jnp.ones((D_INNER,), jnp.float32)
        out_proj_w = jax.random.normal(k3, (D_INNER, D_MODEL), jnp.float32) / np.sqrt(D_INNER)
        return dict(u=u, in_proj_w=in_proj_w, conv_weight=conv_weight, conv_bias=conv_bias, A_log=A_log, dt_bias=dt_bias, D_param=D_param, norm_scale=norm_scale, out_proj_w=out_proj_w)
    _L0_attn_in = _L0_attn_setup()

    def _L0_ffn_setup():
        import jax, jax.numpy as jnp
        import numpy as np
        HIDDEN = 512
        INTER = 2048
        SCALE = 64.0

        def fwht(x):
            orig_shape = x.shape
            n = orig_shape[-1]
            x = x.reshape(-1, n)
            h = 1
            while h < n:
                x = x.reshape(-1, n // (2 * h), 2, h)
                a, b = (x[:, :, 0, :], x[:, :, 1, :])
                x = jnp.stack([a + b, a - b], axis=2).reshape(-1, n)
                h *= 2
            return (x / jnp.sqrt(jnp.asarray(n, x.dtype))).reshape(orig_shape)
        key = jax.random.key(seed)
        ks = jax.random.split(key, 8)
        inp = jax.random.normal(ks[0], (4, 512, HIDDEN), dtype=jnp.float32)
        SU_ug = jnp.where(jax.random.bernoulli(ks[1], 0.5, (HIDDEN,)), 1.0, -1.0).astype(jnp.float32)
        SU_dp = jnp.where(jax.random.bernoulli(ks[2], 0.5, (INTER,)), 1.0, -1.0).astype(jnp.float32)
        Wscale_ug = jax.random.uniform(ks[3], (2 * INTER,), jnp.float32, 0.5, 1.5)
        Wscale_dp = jax.random.uniform(ks[4], (HIDDEN,), jnp.float32, 0.5, 1.5)
        W_up = jax.random.normal(ks[5], (INTER, HIDDEN), dtype=jnp.float32) * 0.02
        W_gate = jax.random.normal(ks[6], (INTER, HIDDEN), dtype=jnp.float32) * 0.02
        W_down = jax.random.normal(ks[7], (HIDDEN, INTER), dtype=jnp.float32) * 0.02
        return {'input': inp, 'SU_ug': SU_ug, 'SU_dp': SU_dp, 'Wscale_ug': Wscale_ug, 'Wscale_dp': Wscale_dp, 'W_up': W_up, 'W_gate': W_gate, 'W_down': W_down}
    _L0_ffn_in = _L0_ffn_setup()
    _d = {'L0_attn_u': _L0_attn_in['u'], 'L0_attn_in_proj_w': _L0_attn_in['in_proj_w'], 'L0_attn_conv_weight': _L0_attn_in['conv_weight'], 'L0_attn_conv_bias': _L0_attn_in['conv_bias'], 'L0_attn_A_log': _L0_attn_in['A_log'], 'L0_attn_dt_bias': _L0_attn_in['dt_bias'], 'L0_attn_D_param': _L0_attn_in['D_param'], 'L0_attn_norm_scale': _L0_attn_in['norm_scale'], 'L0_attn_out_proj_w': _L0_attn_in['out_proj_w'], 'L0_ffn_SU_ug': _L0_ffn_in['SU_ug'], 'L0_ffn_SU_dp': _L0_ffn_in['SU_dp'], 'L0_ffn_Wscale_ug': _L0_ffn_in['Wscale_ug'], 'L0_ffn_Wscale_dp': _L0_ffn_in['Wscale_dp'], 'L0_ffn_W_up': _L0_ffn_in['W_up'], 'L0_ffn_W_gate': _L0_ffn_in['W_gate'], 'L0_ffn_W_down': _L0_ffn_in['W_down']}
    _x0 = _d['L0_attn_u']
    _d['L0_attn_u'] = jax.random.normal(jax.random.fold_in(jax.random.key(seed), 1), (2, 2048, 512), dtype=_x0.dtype)
    del _x0
    return _d

def reference(L0_attn_u, L0_attn_in_proj_w, L0_attn_conv_weight, L0_attn_conv_bias, L0_attn_A_log, L0_attn_dt_bias, L0_attn_D_param, L0_attn_norm_scale, L0_attn_out_proj_w, L0_ffn_SU_ug, L0_ffn_SU_dp, L0_ffn_Wscale_ug, L0_ffn_Wscale_dp, L0_ffn_W_up, L0_ffn_W_gate, L0_ffn_W_down):

    def _L0_attn_ref(u, in_proj_w, conv_weight, conv_bias, A_log, dt_bias, D_param, norm_scale, out_proj_w):
        import jax, jax.numpy as jnp
        import numpy as np
        D_MODEL = 512
        D_STATE = 64
        D_CONV = 4
        EXPAND = 2
        HEADDIM = 64
        NGROUPS = 1
        CHUNK = 64
        D_INNER = D_MODEL * EXPAND
        NHEADS = D_INNER // HEADDIM
        D_IN_PROJ = 2 * D_INNER + 2 * NGROUPS * D_STATE + NHEADS
        BATCH, SEQLEN = (2, 1024)
        RMS_EPS = 1e-06

        def elu_plus_one(x):
            return jax.nn.elu(x) + 1.0

        def softplus(x):
            return jnp.where(x > 20, x, jnp.log1p(jnp.exp(x)))

        def causal_conv1d(x, w, b):
            Bsz, L, Dn = x.shape
            k = w.shape[0]
            xp = jnp.transpose(jnp.pad(x, ((0, 0), (k - 1, 0), (0, 0))), (0, 2, 1))
            kern = jnp.transpose(w, (1, 0))[:, None, :]
            y = jax.lax.conv_general_dilated(xp, kern, (1,), 'VALID', feature_group_count=Dn, dimension_numbers=('NCH', 'OIH', 'NCH'))
            return jnp.transpose(y, (0, 2, 1)) + b

        def ssd_chunked(q, k, v, a, chunk_size):
            Bsz, H, L, N = q.shape
            S = chunk_size
            C = L // S
            qc = q.reshape(Bsz, H, C, S, N)
            kc = k.reshape(Bsz, H, C, S, N)
            vc = v.reshape(Bsz, H, C, S, -1)
            la = jnp.log(a).reshape(Bsz, H, C, S)
            cs = jnp.cumsum(la, axis=-1)
            causal = jnp.tril(jnp.ones((S, S), bool))
            logdec = jnp.where(causal, cs[..., :, None] - cs[..., None, :], -jnp.inf)
            att = jnp.einsum('bhcsn,bhctn->bhcst', qc, kc) * jnp.exp(logdec)
            y_intra = jnp.einsum('bhcst,bhctp->bhcsp', att, vc)
            total = cs[..., -1]
            k_scaled = kc * jnp.exp(total[..., None, None] - cs[..., None])
            states = jnp.einsum('bhcsn,bhcsp->bhcnp', k_scaled, vc)
            d_t = jnp.moveaxis(jnp.exp(total), 2, 0)
            s_t = jnp.moveaxis(states, 2, 0)

            def step(h, inp):
                d, s = inp
                return (d[..., None, None] * h + s, h)
            _, h_prev = jax.lax.scan(step, jnp.zeros_like(s_t[0]), (d_t, s_t))
            h_prev = jnp.moveaxis(h_prev, 0, 2)
            y_inter = jnp.einsum('bhcsn,bhcnp->bhcsp', qc * jnp.exp(cs)[..., None], h_prev)
            return (y_intra + y_inter).reshape(Bsz, H, L, -1)
        Bsz, L, _ = u.shape
        zxBCdt = u @ in_proj_w
        splits = [D_INNER, 2 * D_INNER, 2 * D_INNER + NGROUPS * D_STATE, 2 * D_INNER + 2 * NGROUPS * D_STATE]
        z, x, B_proj, C_proj, dt_logits = jnp.split(zxBCdt, splits, axis=-1)
        x = jax.nn.silu(causal_conv1d(x, conv_weight, conv_bias))
        B_mat = elu_plus_one(B_proj.reshape(Bsz, L, NGROUPS, D_STATE))
        C_mat = elu_plus_one(C_proj.reshape(Bsz, L, NGROUPS, D_STATE))
        hpg = NHEADS // NGROUPS
        B_mat = jnp.repeat(B_mat, hpg, axis=2)
        C_mat = jnp.repeat(C_mat, hpg, axis=2)
        dt = softplus(dt_logits + dt_bias)
        a = jnp.exp(-dt * jnp.exp(A_log))
        x_heads = x.reshape(Bsz, L, NHEADS, HEADDIM)
        q = jnp.transpose(C_mat, (0, 2, 1, 3))
        k = jnp.transpose(B_mat, (0, 2, 1, 3))
        v = jnp.transpose(x_heads, (0, 2, 1, 3))
        a_t = jnp.transpose(a, (0, 2, 1))
        y = ssd_chunked(q, k, v, a_t, CHUNK)
        y = y + D_param[None, :, None, None] * v
        y = jnp.transpose(y, (0, 2, 1, 3)).reshape(Bsz, L, D_INNER)
        y = y * jax.lax.rsqrt(jnp.mean(y * y, axis=-1, keepdims=True) + RMS_EPS) * norm_scale
        y = y * jax.nn.silu(z)
        return y @ out_proj_w

    def _L0_ffn_ref(input, SU_ug, SU_dp, Wscale_ug, Wscale_dp, W_up, W_gate, W_down):
        import jax, jax.numpy as jnp
        import numpy as np
        HIDDEN = 512
        INTER = 2048
        SCALE = 64.0

        def fwht(x):
            orig_shape = x.shape
            n = orig_shape[-1]
            x = x.reshape(-1, n)
            h = 1
            while h < n:
                x = x.reshape(-1, n // (2 * h), 2, h)
                a, b = (x[:, :, 0, :], x[:, :, 1, :])
                x = jnp.stack([a + b, a - b], axis=2).reshape(-1, n)
                h *= 2
            return (x / jnp.sqrt(jnp.asarray(n, x.dtype))).reshape(orig_shape)
        n = SU_ug.shape[0]
        x = input.reshape(-1, n)
        x = fwht(x * SU_ug) / SCALE
        x_up = x @ W_up.T * (Wscale_ug[:INTER] * SCALE)
        x_gate = x @ W_gate.T * (Wscale_ug[INTER:] * SCALE)
        x = jax.nn.silu(x_gate) * x_up
        x = fwht(x * SU_dp) / SCALE
        x = x @ W_down.T * (Wscale_dp * SCALE)
        return x.reshape(input.shape)
    x = L0_attn_u
    xn = _layernorm(x, axis=-1)
    x = x + _L0_attn_ref(xn, L0_attn_in_proj_w, L0_attn_conv_weight, L0_attn_conv_bias, L0_attn_A_log, L0_attn_dt_bias, L0_attn_D_param, L0_attn_norm_scale, L0_attn_out_proj_w) + _L0_ffn_ref(xn, L0_ffn_SU_ug, L0_ffn_SU_dp, L0_ffn_Wscale_ug, L0_ffn_Wscale_dp, L0_ffn_W_up, L0_ffn_W_gate, L0_ffn_W_down)
    return x

_drawn_inputs = setup_inputs


def setup_inputs(seed=0):
    import zlib

    import numpy as np

    out = dict(_drawn_inputs(seed))
    spreads = {'L0_attn_conv_bias': (0.0, 0.1),
     'L0_attn_D_param': (1.0, 0.2),
     'L0_attn_norm_scale': (1.0, 0.2)}
    factors = {}
    for name, (base, spread) in spreads.items():
        noise = np.random.default_rng([zlib.crc32(name.encode()), seed]).standard_normal(out[name].shape)
        drawn = base * np.exp(spread * noise) if base else spread * noise
        out[name] = jnp.asarray(drawn.astype(out[name].dtype))
    for name, factor in factors.items():
        out[name] = (out[name] * factor).astype(out[name].dtype)
    return out
```

```python
import concourse.bass as bass
from concourse import mybir
from contextlib import ExitStack

F32 = mybir.dt.float32
F16 = mybir.dt.float16
I32 = mybir.dt.int32
ALU = mybir.AluOpType
ACT = mybir.ActivationFunctionType

P = 128
BATCH, SEQ, DM = 2, 2048, 512
DI, NS, NH, HD, TAPS = 1024, 64, 16, 64, 4
DPROJ = 2 * DI + 2 * NS + NH
FF = 2048
TB = 256
NT = TB // P
NBLK = SEQ // TB
NBLOCKS = BATCH * NBLK
KD = DM // P
CX = DI // P
KF = FF // P
BC0 = 2 * DI
NBC = 2 * NS + NH
LN_EPS, RMS_EPS = 1e-5, 1e-6
LA_MIN = -1000.0
RSQRT_SEED = float(0x5F3759DF)

TIMELINE = """
bc xp0 xp1 elu cv0 xp2 cv1 xp3 sv0 sv1
F0 qk vt0 cs cv2
F1 G vt1 dq00 dq01 sv2
F2 D0 dec00 cv3
F3 D1 dec01 vt2 sv3
F4 D2 vt3 vw00 dq02 dq03 int00
F5 D3 itr00 dec02
F6 D4 dec03 vw01 int01 st00
F7 D5 itr01 st01 ssq0 dq10 dq11
F8 D6 dec10 z00
F9 D7 z01 dec11 vw10
F10 D8 int10 yt00 yt01
F11 D9 itr10 O0 st10 dq12 dq13
F12 D10 dec12 dec13 vw11 ln
F13 D11 int11 itr11 st11 ssq1
F14 D12 z10
F15 D13 z11 xt0 xt1
D14 yt10 D15 yt11 O1 fin
""".split()

RING_READER = {"bc": "dve", "xp": "act", "qk": "act", "cs": "act", "G": "dve", "vt": "act", "dec": "act",
               "int": "dve", "itr": "dve", "st": "dve", "z": "dve", "yt": "act", "xt": "act"}
BANKS = 4


def kind(step):
    return step.rstrip("0123456789")


def index(step):
    return [int(c) for c in step[len(kind(step)):]]


RING = [s for s in TIMELINE if kind(s) in RING_READER]
NR = len(RING)
NR_ACT = sum(RING_READER[kind(s)] == "act" for s in RING)
NR_DVE = NR - NR_ACT


def filled(step):
    return RING.index(step) + 1


def emptied(step):
    who = RING_READER[kind(step)]
    return sum(RING_READER[kind(s)] == who for s in RING[:RING.index(step) + 1])


def before(step):
    n = RING.index(step)
    if n >= BANKS:
        return RING[n - BANKS], 0
    return [s for m, s in enumerate(RING) if m % BANKS == n][-1], 1


def program(nc, u, in_w, conv_w, conv_b, a_log, dt_bias, d_param, norm_scale, out_w,
            su_ug, su_dp, ws_ug, ws_dp, w_up, w_gate, w_down, out):
    x_v = u.rearrange("b (n t p) d -> (b n) p t d", p=P, t=NT)
    out_v = out.rearrange("b (n t p) d -> (b n) p t d", p=P, t=NT)
    up_v = w_up.rearrange("(g t p) k -> g p t k", t=4, p=P)
    gate_v = w_gate.rearrange("(g t p) k -> g p t k", t=4, p=P)
    down_v = w_down.rearrange("(t p) k -> p t k", p=P)
    GR = FF // DM

    ctx = ExitStack()
    with ctx:
        def sem(name):
            return ctx.enter_context(nc.semaphore(name))

        def sb(name, shape, dt=F32):
            return ctx.enter_context(nc.sbuf_tensor(name, shape, dt))

        banks = [ctx.enter_context(nc.psum_tensor(f"bank{n}", [P, 512], F32)) for n in range(8)]

        wi = sb("wi", [P, KD, DPROJ])
        wug = sb("wug", [P, KD, 2 * FF])
        wd = sb("wd", [P, KF, DM])
        wo = sb("wo", [P, CX, DM])
        cols = sb("cols", [P, 104])
        row3 = sb("row3", [P, 3, NH])
        ident = sb("ident", [P, P])
        upto = sb("upto", [P, P])
        after = sb("after", [P, P])
        ones = sb("ones", [P, P])
        upto16 = sb("upto16", [P, P], F16)
        after16 = sb("after16", [P, P], F16)
        WS_UG, WS_DP, SU_UG, SU_DP, NORM, CONVW, CONVB = 0, 32, 36, 40, 56, 64, 96

        vec_loaded, bcast_loaded, wi_loaded, wo_loaded = (sem(n) for n in ("vec_loaded", "bcast_loaded", "wi_loaded", "wo_loaded"))
        nat_loaded = [sem("nat_loaded0"), sem("nat_loaded1")]
        down_loaded = sem("down_loaded")
        consts_made, cols_filled, cols_ready = sem("consts_made"), sem("cols_filled"), sem("cols_ready")
        had_ready, negexp_ready = sem("had_ready"), sem("negexp_ready")
        nat_scaled, butterfly_done, nat_used = sem("nat_scaled"), sem("butterfly_done"), sem("nat_used")
        wt_filled, wt_copied, hw_filled, hw_stored = sem("wt_filled"), sem("wt_copied"), sem("hw_filled"), sem("hw_stored")
        down_scaled, down_mixed = sem("down_scaled"), sem("down_mixed")
        prepared = sem("prepared")

        with ExitStack() as prep:
            def tmp(name, shape, dt=F32):
                return prep.enter_context(nc.sbuf_tensor(name, shape, dt))

            down_nat = tmp("down_nat", [P, 4, FF])
            nat = [tmp("nat0", [P, 4, DM]), None]
            mix = [tmp("mix0", [P, 4, DM]), None]
            nat[1] = wo[:, 0:4, :]
            mix[1] = wo[:, 4:8, :]
            wt = [tmp(f"wt{n}", [P, 512]) for n in range(2)]
            vec = tmp("vec", [104, P])
            brow = tmp("brow", [1, 3 * NH])
            had = tmp("had", [P, P])
            hi0, hi1, hi2 = (tmp(f"hi{n}", [P, P], I32) for n in range(3))
            down_mix = wd[:, :, :].rearrange("p a n -> p (a n)").rearrange("p (t k) -> p t k", t=4)

            block = ctx.enter_context(nc.Block())

            @block.sync
            def _(sp):
                sp.dma_start(vec[WS_UG:WS_UG + 32, :], ws_ug.rearrange("(r p) -> r p", p=P)).then_inc(vec_loaded, 16)
                sp.dma_start(vec[WS_DP:WS_DP + 4, :], ws_dp.rearrange("(r p) -> r p", p=P)).then_inc(vec_loaded, 16)
                sp.dma_start(vec[SU_UG:SU_UG + 4, :], su_ug.rearrange("(r p) -> r p", p=P)).then_inc(vec_loaded, 16)
                sp.dma_start(vec[SU_DP:SU_DP + 16, :], su_dp.rearrange("(r p) -> r p", p=P)).then_inc(vec_loaded, 16)
                sp.dma_start(vec[NORM:NORM + 8, :], norm_scale.rearrange("(r p) -> r p", p=P)).then_inc(vec_loaded, 16)
                sp.dma_start(vec[CONVW:CONVW + 32, :], conv_w.rearrange("j (r p) -> (j r) p", p=P)).then_inc(vec_loaded, 16)
                sp.dma_start(vec[CONVB:CONVB + 8, :], conv_b.rearrange("(r p) -> r p", p=P)).then_inc(vec_loaded, 16)
                for n, row in enumerate((dt_bias, a_log, d_param)):
                    sp.dma_start(brow[0:1, n * NH:(n + 1) * NH], row.rearrange("(a h) -> a h", a=1)).then_inc(bcast_loaded, 16)
                for g in range(2 * GR):
                    if g >= 2:
                        sp.wait_ge(nat_used, g - 1)
                    sp.dma_start(nat[g % 2][:, :, :], (up_v[g] if g < GR else gate_v[g - GR])).then_inc(nat_loaded[g % 2], 16)
                    if g == 1:
                        sp.dma_start(down_nat[:, :, :], down_v).then_inc(down_loaded, 16)
                sp.dma_start(wi[:, :, :], in_w.rearrange("(a p) n -> p a n", p=P)).then_inc(wi_loaded, 16)
                sp.wait_ge(nat_used, 2 * GR)
                sp.dma_start(wo[:, :, :], out_w.rearrange("(a p) n -> p a n", p=P)).then_inc(wo_loaded, 16)
                sp.sem_inc(prepared, 1)

            @block.gpsimd
            def _(pool):
                pool.memset(ones[:, :], 1.0)
                pool.memset(ident[:, :], 0.0)
                pool.iota(hi0[:, :], [[0, P]], base=0, channel_multiplier=1)
                pool.iota(hi1[:, :], [[1, P]], base=0, channel_multiplier=0).then_inc(consts_made, 1)
                pool.wait_ge(consts_made, 1)
                pool.affine_select(out=ident[:, :], in_=ident[:, :], compare_op=ALU.not_equal, fill=1.0,
                                   base=0, pattern=[[-1, P]], channel_multiplier=1)
                pool.affine_select(out=upto[:, :], in_=ones[:, :], compare_op=ALU.is_ge, fill=0.0,
                                   base=0, pattern=[[1, P]], channel_multiplier=-1)
                pool.affine_select(out=after[:, :], in_=ones[:, :], compare_op=ALU.is_gt, fill=0.0,
                                   base=0, pattern=[[-1, P]], channel_multiplier=1).then_inc(consts_made, 1)
                pool.wait_ge(consts_made, 2)
                pool.tensor_copy(upto16[:, :], upto[:, :])
                pool.tensor_copy(after16[:, :], after[:, :]).then_inc(consts_made, 1)
                pool.wait_ge(down_scaled, 1)
                a, b, h = down_nat, down_mix, 1
                for stage in range(4):
                    if stage:
                        pool.wait_ge(down_mixed, stage)
                    va = a[:, :, :].rearrange("p t (m c w) -> p (t m) c w", c=2, w=h * P)
                    vb = b[:, :, :].rearrange("p t (m c w) -> p (t m) c w", c=2, w=h * P)
                    pool.tensor_tensor(vb[:, :, 0, :], va[:, :, 0, :], va[:, :, 1, :], ALU.add)
                    pool.tensor_tensor(vb[:, :, 1, :], va[:, :, 0, :], va[:, :, 1, :], ALU.subtract).then_inc(down_mixed, 1)
                    a, b, h = b, a, h * 2
                pool.sem_inc(prepared, 1)

            @block.scalar
            def _(act):
                act.wait_ge(vec_loaded, 7 * 16)
                act.wait_ge(bcast_loaded, 3 * 16)
                act.wait_ge(cols_filled, 1)
                nc.scalar.activation(cols[:, 0:104], banks[6][:, 0:104], ACT.Copy)
                nc.scalar.activation(row3[:, 0, :], banks[6][:, 128:128 + NH], ACT.Copy)
                nc.scalar.activation(row3[:, 1, :], banks[6][:, 128 + NH:128 + 2 * NH], ACT.Exp)
                nc.scalar.activation(row3[:, 2, :], banks[6][:, 128 + 2 * NH:128 + 3 * NH], ACT.Copy).then_inc(negexp_ready, 1)
                act.wait_ge(cols_ready, 1)
                act.wait_ge(down_loaded, 16)
                for t in range(4):
                    ins = nc.scalar.activation(down_nat[:, t, :], down_nat[:, t, :], ACT.Copy, scale=cols[:, WS_DP + t:WS_DP + t + 1])
                ins.then_inc(down_scaled, 1)

                def copy_transposed(n):
                    act.wait_ge(wt_filled, n + 1)
                    if n >= 2:
                        act.wait_ge(hw_filled, n - 1)
                    nc.scalar.activation(wt[n % 2][:, :], banks[n % 2][:, :], ACT.Copy).then_inc(wt_copied, 1)

                for g in range(2 * GR):
                    act.wait_ge(nat_loaded[g % 2], 16 * (g // 2 + 1))
                    for t in range(4):
                        ins = nc.scalar.activation(nat[g % 2][:, t, :], nat[g % 2][:, t, :], ACT.Copy, scale=cols[:, 4 * g + t:4 * g + t + 1])
                    ins.then_inc(nat_scaled, 1)
                    if g >= 1:
                        for a in range(KD):
                            copy_transposed((g - 1) * KD + a)
                for n in range((2 * GR - 1) * KD, 2 * GR * KD + KF):
                    copy_transposed(n)
                act.drain().then_inc(prepared, 1)

            @block.vector
            def _(dve):
                dve.wait_ge(consts_made, 1)
                nc.vector.tensor_tensor(hi2[:, :], hi0[:, :], hi1[:, :], ALU.bitwise_and)
                dve.drain()
                for s in (4, 2, 1):
                    nc.vector.tensor_scalar(hi0[:, :], hi2[:, :], s, None, ALU.logical_shift_right)
                    dve.drain()
                    nc.vector.tensor_tensor(hi2[:, :], hi0[:, :], hi2[:, :], ALU.bitwise_xor)
                    dve.drain()
                nc.vector.tensor_scalar(hi0[:, :], hi2[:, :], 1, None, ALU.bitwise_and)
                dve.drain()
                nc.vector.tensor_scalar(had[:, :], hi0[:, :], -2.0, 1.0, ALU.mult, ALU.add).then_inc(had_ready, 1)
                dve.wait_ge(negexp_ready, 1)
                nc.vector.tensor_scalar(row3[:, 1, :], row3[:, 1, :], -1.0, None, ALU.mult)
                nc.vector.tensor_scalar(cols[:, 16:32], cols[:, 16:32], 0.5, None, ALU.mult)
                nc.vector.tensor_scalar(cols[:, SU_UG:SU_UG + 4], cols[:, SU_UG:SU_UG + 4], float(DM) ** -0.5, None, ALU.mult)
                nc.vector.tensor_scalar(cols[:, SU_DP:SU_DP + 16], cols[:, SU_DP:SU_DP + 16], float(FF) ** -0.5, None, ALU.mult)
                nc.vector.tensor_scalar(cols[:, CONVW:104], cols[:, CONVW:104], 0.5, None, ALU.mult).then_inc(cols_ready, 1)
                dve.wait_ge(cols_ready, 1)

                def store_mixed(n):
                    dve.wait_ge(hw_filled, n + 1)
                    g, a = divmod(n, KD)
                    if g < 2 * GR:
                        dst, sc = wug[:, a, g * 512:(g + 1) * 512], cols[:, SU_UG + a:SU_UG + a + 1]
                    else:
                        a = n - 2 * GR * KD
                        dst, sc = wd[:, a, :], cols[:, SU_DP + a:SU_DP + a + 1]
                    nc.vector.tensor_scalar(dst, banks[2 + n % 2][:, :], sc, None, ALU.mult).then_inc(hw_stored, 1)

                for g in range(2 * GR):
                    dve.wait_ge(nat_scaled, g + 1)
                    for stage, (src, dst) in enumerate(((nat[g % 2], mix[g % 2]), (mix[g % 2], nat[g % 2]))):
                        w = P << stage
                        vs = src[:, :, :].rearrange("p t (m c w) -> p (t m) c w", c=2, w=w)
                        vd = dst[:, :, :].rearrange("p t (m c w) -> p (t m) c w", c=2, w=w)
                        nc.vector.tensor_tensor(vd[:, :, 0, :], vs[:, :, 0, :], vs[:, :, 1, :], ALU.add)
                        ins = nc.vector.tensor_tensor(vd[:, :, 1, :], vs[:, :, 0, :], vs[:, :, 1, :], ALU.subtract)
                        if stage == 0:
                            dve.drain()
                    ins.then_inc(butterfly_done, 1)
                    if g >= 1:
                        for a in range(KD):
                            store_mixed((g - 1) * KD + a)
                for n in range((2 * GR - 1) * KD, 2 * GR * KD + KF):
                    store_mixed(n)
                dve.wait_ge(wo_loaded, 16)
                for t in range(CX):
                    nc.vector.tensor_scalar(wo[:, t, :], wo[:, t, :], cols[:, NORM + t:NORM + t + 1], None, ALU.mult)
                dve.drain().then_inc(prepared, 1)

            @block.tensor
            def _(pe):
                pe.wait_ge(consts_made, 2)
                pe.wait_ge(vec_loaded, 7 * 16)
                nc.tensor.transpose(banks[6][:, 0:104], vec[:, :], ident[0:104, 0:104])
                pe.wait_ge(bcast_loaded, 3 * 16)
                nc.tensor.matmul(banks[6][:, 128:128 + 3 * NH], ones[0:1, :], brow[0:1, :], start=True, stop=True).then_inc(cols_filled, 1)
                pe.wait_ge(had_ready, 1)

                def transposes(n):
                    g, a = divmod(n, KD)
                    if g < 2 * GR:
                        if a == 0:
                            pe.wait_ge(butterfly_done, g + 1)
                        src = nat[g % 2]
                    else:
                        a = n - 2 * GR * KD
                        pe.wait_ge(down_mixed, 4)
                        src = down_nat
                    if n >= 2:
                        pe.wait_ge(wt_copied, n - 1)
                    for t in range(4):
                        ins = nc.tensor.transpose(banks[n % 2][:, t * P:(t + 1) * P], src[:, t, a * P:(a + 1) * P], ident[:, :])
                    ins.then_inc(wt_filled, 1)
                    if g < 2 * GR and a == KD - 1:
                        pe.wait_ge(wt_filled, n + 1)
                        pe.sem_inc(nat_used, 1)

                def hadamard(n):
                    pe.wait_ge(wt_copied, n + 1)
                    if n >= 2:
                        pe.wait_ge(hw_stored, n - 1)
                    nc.tensor.matmul(banks[2 + n % 2][:, :], had[:, :], wt[n % 2][:, :], start=True, stop=True).then_inc(hw_filled, 1)

                total = 2 * GR * KD + KF
                transposes(0)
                for n in range(total):
                    if n + 1 < total:
                        transposes(n + 1)
                    hadamard(n)
                pe.sem_inc(prepared, 1)

        stats = sb("stats", [P, NT, 6])
        mv = sb("mv", [P, NT, 2])
        rs = sb("rs", [P, 4, NT])
        xnT = sb("xnT", [P, KD, TB])
        xc = [sb(f"xc{n}", [P, 2, TAPS - 1 + TB]) for n in range(2)]
        halo = sb("halo", [P, CX, TAPS - 1])
        cvx = sb("cvx", [P, 2, 2, TB])
        cv = [cvx[:, n, :, :] for n in range(2)]
        xin = cvx[:, :, :, :].rearrange("p a c t -> p a (c t)")
        ctz = sb("ctz", [P, 512])
        ct = ctz[:, :].rearrange("p (c t) -> p c t", c=2)
        zt = ctz
        junk = ctz[:, :].bitcast(F16)
        raw = sb("raw", [P, NT, NBC])
        neg = sb("neg", [P, NT, NBC])
        kq = sb("kq", [P, NT, 2 * NS])
        lns = sb("lns", [P, NT, NH])
        la = sb("la", [P, NT, NH])
        la16 = sb("la16", [P, 2, NT, NH], F16)
        qkT = sb("qkT", [NS, 2, NT, P])
        dec3 = sb("dec3", [P, 3, NT, NH])
        Gm = sb("Gm", [P, NT, P])
        v = sb("v", [P, NT, DI])
        dr = [sb(f"dr{n}", [P, 2, 4, P], F16) for n in range(2)]
        Mx = sb("Mx", [P, 2, 4, P])
        M = [Mx[:, n, :, :] for n in range(2)]
        res = Mx[:, :, :, :].rearrange("p a h s -> p a (h s)")
        yi = sb("yi", [P, 512])
        vw = [sb(f"vw{n}", [P, 512]) for n in range(2)]
        vd = sb("vd", [P, 512])
        state = sb("state", [NS, DI])
        ssq = sb("ssq", [P, NT])
        yT = sb("yT", [P, CX, P])
        tg = [sb(f"tg{n}", [P, TB]) for n in range(2)]
        h = [sb(f"h{n}", [P, TB]) for n in range(3)]

        ring = banks[0:BANKS]
        ug = banks[4:6]
        acc = banks[6:8]

        ring_filled, act_emptied, dve_emptied = sem("ring_filled"), sem("act_emptied"), sem("dve_emptied")
        ug_filled, ug_emptied, h_ready, h_used = sem("ug_filled"), sem("ug_emptied"), sem("h_ready"), sem("h_used")
        acc_filled, acc_emptied = sem("acc_filled"), sem("acc_emptied")
        tanh_gate, tanh_conv, tanh_z = sem("tanh_gate"), sem("tanh_conv"), sem("tanh_z")
        raw_ready, exps_done, ln_done, kq_ready = sem("raw_ready"), sem("exps_done"), sem("ln_done"), sem("kq_ready")
        conv_done, vT_ready, dr_ready, M_ready = sem("conv_done"), sem("vT_ready"), sem("dr_ready"), sem("M_ready")
        state_ready, vw_ready, y_ready, ssq_ready, yg_ready = (sem(n) for n in ("state_ready", "vw_ready", "y_ready", "ssq_ready", "yg_ready"))
        xn_ready, out_ready = sem("xn_ready"), sem("out_ready")
        x_loaded, res_loaded, out_stored = sem("x_loaded"), sem("res_loaded"), sem("out_stored")

        def position(step):
            return ring[RING.index(step) % BANKS]

        def bcast(ap, n):
            return ap.unsqueeze(len(ap.shape)).to_broadcast(list(ap.shape) + [n])

        @block.sync
        def _(sp):
            sp.wait_ge(prepared, 5)
            sp.dma_start(xin[:, :, :], x_v[0]).then_inc(x_loaded, 16)

            def step(i, following):
                sp.wait_ge(ring_filled, (i + 1) * NR + filled("vt3"))
                sp.dma_start(xin[:, :, :], x_v[following]).then_inc(x_loaded, 16)
                sp.wait_ge(ring_filled, (i + 1) * NR + filled("itr11"))
                sp.dma_start(res[:, :, :], x_v[i]).then_inc(res_loaded, 16)
                sp.wait_ge(out_ready, (i + 1) * NT)
                sp.dma_start(out_v[i], res[:, :, :]).then_inc(out_stored, 16)

            sp.sem_inc(out_stored, 16)
            with sp.Fori(0, NBLOCKS - 1) as i:
                step(i, i + 1)
            step(NBLOCKS - 1, 0)
            sp.wait_ge(x_loaded, 16 * (NBLOCKS + 1))
            sp.wait_ge(out_stored, 16 * (NBLOCKS + 1))

        @block.tensor
        def _(pe):
            pe.sem_inc(ring_filled, filled("xt0") - 1)
            for s, k in ((ug_filled, KF), (h_used, KF), (acc_filled, 1)):
                pe.sem_inc(s, k)
            pe.wait_ge(prepared, 5)

            def bank(i, s):
                prior, ago = before(s)
                reader, count = (act_emptied, NR_ACT) if RING_READER[kind(prior)] == "act" else (dve_emptied, NR_DVE)
                pe.wait_ge(reader, (i + 1 - ago) * count + emptied(prior))
                return position(s)

            def transpose_x(i, s):
                j, = index(s)
                pe.wait_ge(xn_ready, (i + 1) * NT + j + 1)
                o = bank(i, s)
                for a in range(KD):
                    ins = nc.tensor.transpose(o[:, a * P:(a + 1) * P], xin[:, j, a * P:(a + 1) * P], ident[:, :])
                ins.then_inc(ring_filled, 1)

            def products(out, pairs, first=True, last=True):
                for n, (lhsT, rhs) in enumerate(pairs):
                    ins = nc.tensor.matmul(out, lhsT, rhs, start=first and n == 0, stop=last and n == len(pairs) - 1)
                return ins

            def body(i):
                for s in TIMELINE:
                    k, at = kind(s), index(s)
                    if k == "bc":
                        pe.wait_ge(act_emptied, i * NR_ACT + emptied("xt1"))
                        o = bank(i, s)
                        for j in range(NT):
                            ins = products(o[:, j * NBC:(j + 1) * NBC],
                                           [(xnT[:, a, j * P:(j + 1) * P], wi[:, a, BC0:DPROJ]) for a in range(KD)])
                        ins.then_inc(ring_filled, 1)
                    elif k == "xp":
                        o = bank(i, s)
                        for c in range(2):
                            col = DI + (2 * at[0] + c) * P
                            ins = products(o[:, c * TB:(c + 1) * TB],
                                           [(wi[:, a, col:col + P], xnT[:, a, :]) for a in range(KD)])
                        ins.then_inc(ring_filled, 1)
                    elif k == "F":
                        c = at[0] if len(at) == 1 else 10 * at[0] + at[1]
                        pe.wait_ge(ug_emptied, (i + 1) * KF + c - 1)
                        for n, col in enumerate((FF + c * P, c * P)):
                            ins = products(ug[c % 2][:, n * TB:(n + 1) * TB],
                                           [(wug[:, a, col:col + P], xnT[:, a, :]) for a in range(KD)])
                        ins.then_inc(ug_filled, 1)
                    elif k == "D":
                        c = at[0] if len(at) == 1 else 10 * at[0] + at[1]
                        if c == 0:
                            pe.wait_ge(acc_emptied, i + 1)
                        pe.wait_ge(h_ready, (i + 1) * KF + c + 1)
                        for j in range(NT):
                            ins = products(acc[j][:, :], [(h[c % 3][:, j * P:(j + 1) * P], wd[:, c, :])],
                                           first=c == 0, last=c == KF - 1 and j == 0)
                        ins.then_inc(h_used, 1)
                    elif k == "qk":
                        pe.wait_ge(kq_ready, i + 2)
                        o = bank(i, s)
                        for n in range(2):
                            for j in range(NT):
                                ins = products(o[0:NS, (n * NT + j) * P:(n * NT + j + 1) * P],
                                               [(kq[:, j, n * NS:(n + 1) * NS], ident[:, :])])
                        ins.then_inc(ring_filled, 1)
                    elif k == "cs":
                        o = bank(i, s)
                        for n, w in enumerate((upto, after, ones)):
                            ins = products(o[:, n * NT * NH:(n + 1) * NT * NH],
                                           [(w[:, :], la[:, :, :].rearrange("p t h -> p (t h)"))])
                        ins.then_inc(ring_filled, 1)
                    elif k == "G":
                        pe.wait_ge(act_emptied, (i + 1) * NR_ACT + emptied("qk"))
                        o = bank(i, s)
                        for j in range(NT):
                            ins = products(o[:, j * P:(j + 1) * P], [(qkT[:, 0, j, :], qkT[:, 1, j, :])])
                        ins.then_inc(ring_filled, 1)
                    elif k == "vt":
                        pe.wait_ge(vT_ready, (i + 1) * 4 + at[0] + 1)
                        o = bank(i, s)
                        for j in range(NT):
                            for c in range(2):
                                ins = nc.tensor.transpose(o[:, (2 * j + c) * P:(2 * j + c + 1) * P],
                                                          cv[at[0] % 2][:, c, j * P:(j + 1) * P], ident[:, :])
                        ins.then_inc(ring_filled, 1)
                    elif k == "dec":
                        c, q = at
                        pe.wait_ge(dr_ready, (i + 1) * 8 + 4 * c + q + 1)
                        o = bank(i, s)
                        products(o[:, :], [(after16[:, :], dr[q % 2][:, n, :, :].rearrange("p h s -> p (h s)"))
                                           for n in range(2)]).then_inc(ring_filled, 1)
                    elif k == "int":
                        c, hf = at
                        pe.wait_ge(state_ready, (i + 1) * 4 + 2 * c + hf - 1)
                        o = bank(i, s)
                        products(o[:, :], [(qkT[:, 1, c, :], state[:, hf * 512:(hf + 1) * 512])]).then_inc(ring_filled, 1)
                    elif k == "itr":
                        c, hf = at
                        pe.wait_ge(M_ready, (i + 1) * 8 + 4 * c + 2 * hf + 2)
                        pe.wait_ge(act_emptied, (i + 1) * NR_ACT + emptied("vt3"))
                        o = bank(i, s)
                        for n in range(8):
                            hd = 8 * hf + n
                            ins = products(o[:, n * HD:(n + 1) * HD],
                                           [(M[n // 4][:, n % 4, :], v[:, c, hd * HD:(hd + 1) * HD])])
                        ins.then_inc(ring_filled, 1)
                    elif k == "st":
                        c, hf = at
                        pe.wait_ge(vw_ready, (i + 1) * 4 + 2 * c + hf + 1)
                        o = bank(i, s)
                        products(o[0:NS, :], [(kq[:, c, 0:NS], vw[hf][:, :])]).then_inc(ring_filled, 1)
                    elif k == "z":
                        c, hf = at
                        o = bank(i, s)
                        products(o[:, :], [(xnT[:, a, c * P:(c + 1) * P], wi[:, a, hf * 512:(hf + 1) * 512])
                                           for a in range(KD)]).then_inc(ring_filled, 1)
                    elif k == "yt":
                        c, hf = at
                        pe.wait_ge(yg_ready, (i + 1) * 4 + 2 * c + hf + 1)
                        o = bank(i, s)
                        for n in range(4):
                            ins = nc.tensor.transpose(o[:, n * P:(n + 1) * P], v[:, c, (4 * hf + n) * P:(4 * hf + n + 1) * P], ident[:, :])
                        ins.then_inc(ring_filled, 1)
                    elif k == "O":
                        c = at[0]
                        pe.wait_ge(act_emptied, (i + 1) * NR_ACT + emptied(f"yt{c}1"))
                        ins = products(acc[c][:, :], [(yT[:, a, :], wo[:, a, :]) for a in range(CX)],
                                       first=False, last=c == NT - 1)
                        if c == NT - 1:
                            ins.then_inc(acc_filled, 1)
                    elif k == "xt":
                        transpose_x(i, s)

            transpose_x(-1, "xt0")
            transpose_x(-1, "xt1")
            pe.wait_ge(ring_filled, filled("xt1"))
            pe.sem_inc(ring_filled, NR - filled("xt1"))
            with pe.Fori(0, NBLOCKS) as i:
                body(i)

        @block.scalar
        def _(act):
            act.sem_inc(act_emptied, emptied("xt0") - 1)
            for s, k in ((tanh_gate, KF), (tanh_conv, 4), (tanh_z, 4), (exps_done, 1), (ln_done, 1), (ssq_ready, NT)):
                act.sem_inc(s, k)
            act.wait_ge(prepared, 5)

            def copy_xn(i, s):
                j, = index(s)
                act.wait_ge(ring_filled, (i + 1) * NR + filled(s))
                nc.scalar.activation(xnT[:, :, j * P:(j + 1) * P],
                                     position(s)[:, :].rearrange("p (a t) -> p a t", a=KD), ACT.Copy).then_inc(act_emptied, 1)

            def body(i):
                def ring_has(s):
                    act.wait_ge(ring_filled, (i + 1) * NR + filled(s))
                    return position(s)

                for s in TIMELINE:
                    k, at = kind(s), index(s)
                    if k == "xp":
                        o = ring_has(s)
                        act.wait_ge(conv_done, (i + 1) * 4 + at[0] - 1)
                        nc.scalar.activation(xc[at[0] % 2][:, :, TAPS - 1:],
                                             o[:, :].rearrange("p (c t) -> p c t", c=2), ACT.Copy).then_inc(act_emptied, 1)
                    elif k == "elu":
                        act.wait_ge(raw_ready, i + 2)
                        nc.scalar.activation(neg[:, :, :], neg[:, :, :], ACT.Exp).then_inc(exps_done, 1)
                        act.drain()
                        nc.scalar.activation(lns[:, :, :], neg[:, :, 2 * NS:], ACT.Ln, bias=1.0).then_inc(ln_done, 1)
                    elif k == "sv":
                        act.wait_ge(conv_done, (i + 1) * 4 + at[0] + 1)
                        act.wait_ge(vT_ready, (i + 1) * 4 + at[0])
                        act.wait_ge(yg_ready, (i + 1) * 4)
                        nc.scalar.activation(ct[:, :, :], cv[at[0] % 2][:, :, :], ACT.Tanh).then_inc(tanh_conv, 1)
                    elif k == "F":
                        c = at[0] if len(at) == 1 else 10 * at[0] + at[1]
                        act.wait_ge(ug_filled, (i + 1) * KF + c + 1)
                        act.wait_ge(ug_emptied, (i + 1) * KF + c - 1)
                        nc.scalar.activation(tg[c % 2][:, :], ug[c % 2][:, 0:TB], ACT.Tanh).then_inc(tanh_gate, 1)
                    elif k == "qk":
                        o = ring_has(s)
                        nc.scalar.activation(qkT[:, :, :, :].rearrange("n a t p -> n (a t p)"), o[0:NS, :], ACT.Copy).then_inc(act_emptied, 1)
                    elif k == "cs":
                        o = ring_has(s)
                        act.wait_ge(dve_emptied, i * NR_DVE + emptied("st11"))
                        act.wait_ge(vw_ready, (i + 1) * 4)
                        nc.scalar.activation(dec3[:, :, :, :].rearrange("p a t h -> p (a t h)"), o[:, 0:3 * NT * NH], ACT.Exp).then_inc(act_emptied, 1)
                    elif k == "vt":
                        o = ring_has(s)
                        nc.scalar.activation(v[:, :, 2 * at[0] * P:(2 * at[0] + 2) * P],
                                             o[:, :].rearrange("p (t c) -> p t c", t=NT), ACT.Copy).then_inc(act_emptied, 1)
                    elif k == "dec":
                        c, q = at
                        o = ring_has(s)
                        if c == 0 and q < 2:
                            act.wait_ge(out_stored, (i + 1) * 16)
                        else:
                            act.wait_ge(ring_filled, (i + 1) * NR + filled(f"itr{(4 * c + q - 2) // 4}{(4 * c + q - 2) % 4 // 2}"))
                        nc.scalar.activation(M[q % 2][:, :, :].rearrange("p h s -> p (h s)"), o[:, :], ACT.Exp).then_inc(act_emptied, 1)
                    elif k == "ssq":
                        act.drain()
                        act.wait_ge(y_ready, (i + 1) * 4 + 2 * at[0] + 2)
                        act.wait_ge(yg_ready, (i + 1) * 4 + 2 * at[0])
                        nc.scalar.activation(junk[:, :], v[:, at[0], :], ACT.Square, accum_out=ssq[:, at[0]:at[0] + 1]).then_inc(ssq_ready, 1)
                    elif k == "z":
                        act.drain()
                        o = ring_has(s)
                        act.wait_ge(yg_ready, (i + 1) * 4 + 2 * at[0] + at[1])
                        nc.scalar.activation(zt[:, :], o[:, :], ACT.Tanh, scale=0.5).then_inc(tanh_z, 1)
                    elif k == "yt":
                        o = ring_has(s)
                        nc.scalar.activation(yT[:, 4 * at[1]:4 * at[1] + 4, :],
                                             o[:, :].rearrange("p (a t) -> p a t", a=4), ACT.Copy).then_inc(act_emptied, 1)
                    elif k == "xt":
                        copy_xn(i, s)

            copy_xn(-1, "xt0")
            copy_xn(-1, "xt1")
            act.wait_ge(act_emptied, emptied("xt1"))
            act.sem_inc(act_emptied, NR_ACT - emptied("xt1"))
            with act.Fori(0, NBLOCKS) as i:
                body(i)

        @block.gpsimd
        def _(pool):
            for s, k in ((dr_ready, 8), (vw_ready, 4)):
                pool.sem_inc(s, k)
            pool.wait_ge(prepared, 5)
            with pool.Fori(0, NBLOCKS) as i:
                for s in TIMELINE:
                    k, at = kind(s), index(s)
                    if k == "dq":
                        c, q = at
                        if c == 0 and q == 0:
                            pool.wait_ge(kq_ready, i + 2)
                        if c == 0 and q < 2:
                            pool.wait_ge(ring_filled, i * NR + filled(f"dec1{q + 2}"))
                        else:
                            pool.wait_ge(ring_filled, (i + 1) * NR + filled(f"dec{(4 * c + q - 2) // 4}{(4 * c + q - 2) % 4}"))
                        pool.tensor_tensor(dr[q % 2][:, :, :, :], bcast(la16[:, :, c, 4 * q:4 * q + 4], P),
                                           upto16[:, :].unsqueeze(1).unsqueeze(1).to_broadcast([P, 2, 4, P]),
                                           ALU.mult).then_inc(dr_ready, 1)
                    elif k == "vw":
                        c, hf = at
                        pool.wait_ge(act_emptied, (i + 1) * NR_ACT + emptied("vt3"))
                        if c == 0:
                            pool.wait_ge(ring_filled, i * NR + filled(f"st1{hf}"))
                        else:
                            pool.wait_ge(ring_filled, (i + 1) * NR + filled(f"st0{hf}"))
                        n = 2 * c + hf
                        if n == 0:
                            pool.wait_ge(dve_emptied, i * NR_DVE + emptied("int11"))
                        else:
                            pool.wait_ge(dve_emptied, (i + 1) * NR_DVE + emptied(f"int{(n - 1) // 2}{(n - 1) % 2}"))
                        vh = v[:, c, hf * 512:(hf + 1) * 512].rearrange("p (h d) -> p h d", d=HD)
                        pool.tensor_tensor(vw[hf][:, :].rearrange("p (h d) -> p h d", d=HD), vh,
                                           bcast(dec3[:, 1, c, 8 * hf:8 * hf + 8], HD), ALU.mult)
                        pool.tensor_tensor(vd[:, :].rearrange("p (h d) -> p h d", d=HD), vh,
                                           bcast(row3[:, 2, 8 * hf:8 * hf + 8], HD), ALU.mult).then_inc(vw_ready, 1)

        @block.vector
        def _(dve):
            dve.sem_inc(dve_emptied, NR_DVE)
            for s, k in ((ug_emptied, KF), (h_ready, KF), (acc_emptied, 1), (raw_ready, 1), (kq_ready, 1), (conv_done, 4),
                         (vT_ready, 4), (M_ready, 8), (state_ready, 4), (y_ready, 4), (yg_ready, 4)):
                dve.sem_inc(s, k)
            dve.wait_ge(prepared, 5)

            def rsqrt(x, y, a):
                nc.vector.tensor_scalar(a.bitcast(I32), x.bitcast(I32), 1, None, ALU.logical_shift_right)
                dve.drain()
                nc.vector.tensor_scalar(y.bitcast(I32), a.bitcast(I32), -1.0, RSQRT_SEED, ALU.mult, ALU.add)
                dve.drain()
                for _ in range(3):
                    nc.vector.tensor_tensor(a, y, y, ALU.mult)
                    dve.drain()
                    nc.vector.scalar_tensor_tensor(a, a, -0.5, x, ALU.mult, ALU.mult)
                    dve.drain()
                    nc.vector.scalar_tensor_tensor(y, a, 1.5, y, ALU.add, ALU.mult)
                    dve.drain()

            def layer_norm(i):
                dve.wait_ge(x_loaded, (i + 2) * 16)
                for j in range(NT):
                    nc.vector.bn_stats(stats[:, j, :], xin[:, j, :])
                dve.drain()
                for j in range(NT):
                    nc.vector.bn_aggr(mv[:, j, :], stats[:, j, :])
                dve.drain()
                nc.vector.tensor_scalar(rs[:, 0, :], mv[:, :, 1], 1.0, LN_EPS, ALU.mult, ALU.add)
                dve.drain()
                rsqrt(rs[:, 0, :], rs[:, 1, :], rs[:, 2, :])
                for j in range(NT):
                    nc.vector.tensor_scalar(xin[:, j, :], xin[:, j, :], mv[:, j, 0:1], rs[:, 1, j:j + 1],
                                            ALU.subtract, ALU.mult).then_inc(xn_ready, 1)

            def body(i):
                def ring_has(s):
                    dve.wait_ge(ring_filled, (i + 1) * NR + filled(s))
                    return position(s)

                for s in TIMELINE:
                    k, at = kind(s), index(s)
                    if k == "bc":
                        o = ring_has(s)
                        nc.vector.tensor_copy(raw[:, :, :], o[:, 0:NT * NBC].rearrange("p (t n) -> p t n", t=NT)).then_inc(dve_emptied, 1)
                        dve.drain()
                        nc.vector.tensor_tensor(raw[:, :, 2 * NS:], raw[:, :, 2 * NS:], row3[:, 0, :].unsqueeze(1).to_broadcast([P, NT, NH]), ALU.add)
                        nc.vector.tensor_scalar(neg[:, :, 0:2 * NS], raw[:, :, 0:2 * NS], 0.0, None, ALU.min)
                        dve.drain()
                        nc.vector.scalar_tensor_tensor(neg[:, :, 2 * NS:], raw[:, :, 2 * NS:], -1.0, raw[:, :, 2 * NS:], ALU.mult, ALU.min).then_inc(raw_ready, 1)
                    elif k == "elu":
                        dve.wait_ge(exps_done, i + 2)
                        nc.vector.scalar_tensor_tensor(kq[:, :, :], raw[:, :, 0:2 * NS], 0.0, neg[:, :, 0:2 * NS], ALU.max, ALU.add)
                        dve.wait_ge(ln_done, i + 2)
                        nc.vector.scalar_tensor_tensor(lns[:, :, :], raw[:, :, 2 * NS:], 0.0, lns[:, :, :], ALU.max, ALU.add)
                        dve.drain()
                        nc.vector.tensor_tensor(la[:, :, :], lns[:, :, :], row3[:, 1, :].unsqueeze(1).to_broadcast([P, NT, NH]), ALU.mult)
                        dve.drain()
                        nc.vector.tensor_scalar(la[:, :, :], la[:, :, :], LA_MIN, None, ALU.max)
                        dve.drain()
                        nc.vector.tensor_copy(la16[:, 0, :, :], la[:, :, :])
                        dve.drain()
                        nc.vector.tensor_tensor(la16[:, 1, :, :], la[:, :, :], la16[:, 0, :, :], ALU.subtract).then_inc(kq_ready, 1)
                    elif k == "cv":
                        n = at[0]
                        dve.wait_ge(act_emptied, (i + 1) * NR_ACT + emptied(f"xp{n}"))
                        dve.wait_ge(ring_filled, (i + 1) * NR + (0 if n < 2 else filled(f"vt{n - 2}")))
                        x = xc[n % 2]
                        nc.vector.tensor_copy(x[:, :, 0:TAPS - 1], halo[:, 2 * n:2 * n + 2, :])
                        for c in range(2):
                            t = 2 * n + c
                            nc.vector.tensor_scalar(cv[n % 2][:, c, :], x[:, c, 3:3 + TB], cols[:, CONVW + 24 + t:CONVW + 25 + t],
                                                    cols[:, CONVB + t:CONVB + t + 1], ALU.mult, ALU.add)
                        for j in range(3):
                            dve.drain()
                            for c in range(2):
                                t = 2 * n + c
                                ins = nc.vector.scalar_tensor_tensor(cv[n % 2][:, c, :], x[:, c, j:j + TB],
                                                                     cols[:, CONVW + 8 * j + t:CONVW + 8 * j + t + 1],
                                                                     cv[n % 2][:, c, :], ALU.mult, ALU.add)
                        nc.vector.tensor_copy(halo[:, 2 * n:2 * n + 2, :], x[:, :, TB:TB + TAPS - 1]).then_inc(conv_done, 1)
                    elif k == "sv":
                        n = at[0]
                        dve.wait_ge(tanh_conv, (i + 1) * 4 + n + 1)
                        nc.vector.scalar_tensor_tensor(cv[n % 2][:, :, :], ct[:, :, :], 1.0, cv[n % 2][:, :, :], ALU.add, ALU.mult).then_inc(vT_ready, 1)
                    elif k == "F":
                        c = at[0] if len(at) == 1 else 10 * at[0] + at[1]
                        dve.wait_ge(tanh_gate, (i + 1) * KF + c + 1)
                        nc.vector.scalar_tensor_tensor(tg[c % 2][:, :], tg[c % 2][:, :], 1.0, ug[c % 2][:, 0:TB], ALU.add, ALU.mult)
                        dve.drain()
                        dve.wait_ge(h_used, (i + 1) * KF + c - 2)
                        nc.vector.tensor_tensor(h[c % 3][:, :], ug[c % 2][:, TB:2 * TB], tg[c % 2][:, :], ALU.mult).then_inc(h_ready, 1)
                        dve.wait_ge(h_ready, (i + 1) * KF + c + 1)
                        dve.sem_inc(ug_emptied, 1)
                    elif k == "G":
                        o = ring_has(s)
                        nc.vector.tensor_tensor(Gm[:, :, :], o[:, 0:NT * P].rearrange("p (t s) -> p t s", t=NT),
                                                upto[:, :].unsqueeze(1).to_broadcast([P, NT, P]), ALU.mult).then_inc(dve_emptied, 1)
                    elif k == "dec":
                        c, q = at
                        dve.drain()
                        dve.wait_ge(act_emptied, (i + 1) * NR_ACT + emptied(s))
                        nc.vector.tensor_tensor(M[q % 2][:, :, :], M[q % 2][:, :, :],
                                                Gm[:, c, :].unsqueeze(1).to_broadcast([P, 4, P]), ALU.mult).then_inc(M_ready, 1)
                    elif k == "int":
                        c, hf = at
                        o = ring_has(s)
                        nc.vector.tensor_tensor(yi[:, :].rearrange("p (h d) -> p h d", d=HD), o[:, :].rearrange("p (h d) -> p h d", d=HD),
                                                bcast(dec3[:, 0, c, 8 * hf:8 * hf + 8], HD), ALU.mult)
                        dve.drain()
                        dve.wait_ge(vw_ready, (i + 1) * 4 + 2 * c + hf + 1)
                        nc.vector.tensor_tensor(yi[:, :], yi[:, :], vd[:, :], ALU.add).then_inc(dve_emptied, 1)
                    elif k == "itr":
                        c, hf = at
                        dve.drain()
                        o = ring_has(s)
                        ins = nc.vector.tensor_tensor(v[:, c, hf * 512:(hf + 1) * 512], o[:, :], yi[:, :], ALU.add)
                        ins.then_inc(y_ready, 1)
                        dve.wait_ge(y_ready, (i + 1) * 4 + 2 * c + hf + 1)
                        dve.sem_inc(dve_emptied, 1)
                    elif k == "st":
                        c, hf = at
                        half = state[:, hf * 512:(hf + 1) * 512]
                        o = ring_has(s)
                        nc.vector.tensor_tensor(half.rearrange("p (h d) -> p h d", d=HD), half.rearrange("p (h d) -> p h d", d=HD),
                                                bcast(dec3[0:NS, 2, c, 8 * hf:8 * hf + 8], HD), ALU.mult)
                        dve.drain()
                        nc.vector.tensor_tensor(half, o[0:NS, :], half, ALU.add).then_inc(state_ready, 1)
                        dve.wait_ge(state_ready, (i + 1) * 4 + 2 * c + hf + 1)
                        dve.sem_inc(dve_emptied, 1)
                    elif k == "ssq":
                        dve.wait_ge(ssq_ready, (i + 1) * NT + at[0] + 1)
                        c = slice(at[0], at[0] + 1)
                        nc.vector.tensor_scalar(rs[:, 0, c], ssq[:, c], 1.0 / DI, RMS_EPS, ALU.mult, ALU.add)
                        dve.drain()
                        rsqrt(rs[:, 0, c], rs[:, 3, c], rs[:, 2, c])
                        nc.vector.tensor_scalar(rs[:, 3, c], rs[:, 3, c], 0.5, None, ALU.mult)
                        dve.drain()
                    elif k == "z":
                        c, hf = at
                        dve.wait_ge(tanh_z, (i + 1) * 4 + 2 * c + hf + 1)
                        nc.vector.scalar_tensor_tensor(zt[:, :], zt[:, :], 1.0, position(s)[:, :], ALU.add, ALU.mult).then_inc(dve_emptied, 1)
                        dve.drain()
                        vh = v[:, c, hf * 512:(hf + 1) * 512]
                        nc.vector.scalar_tensor_tensor(vh, vh, rs[:, 3, c:c + 1], zt[:, :], ALU.mult, ALU.mult).then_inc(yg_ready, 1)
                    elif k == "ln":
                        layer_norm(i)
                    elif k == "fin":
                        dve.wait_ge(res_loaded, (i + 1) * 16)
                        dve.wait_ge(acc_filled, i + 2)
                        for j in range(NT):
                            nc.vector.tensor_tensor(res[:, j, :], acc[j][:, :], res[:, j, :], ALU.add).then_inc(out_ready, 1)
                        dve.wait_ge(out_ready, (i + 1) * NT)
                        dve.sem_inc(acc_emptied, 1)

            layer_norm(-1)
            with dve.Fori(0, BATCH) as b:
                nc.vector.memset(state[:, :], 0.0)
                nc.vector.memset(halo[:, :, :], 0.0)
                dve.drain()
                with dve.Fori(0, NBLK) as j:
                    body(b * NBLK + j)


_INS = ["u", "in_proj_w", "conv_weight", "conv_bias", "A_log", "dt_bias", "D_param", "norm_scale", "out_proj_w"]
_FFN = ["SU_ug", "SU_dp", "Wscale_ug", "Wscale_dp", "W_up", "W_gate", "W_down"]


def kernel(**inputs):
    import numpy as _np
    import concourse.bacc as _bacc
    from concourse import mybir as _mybir
    from concourse.bass_utils import run_bass_kernel_spmd as _run

    nc = _bacc.Bacc("TRN2", target_bir_lowering=False, num_devices=1)
    arrays, args = {}, []
    for name in [f"L0_attn_{n}" for n in _INS] + [f"L0_ffn_{n}" for n in _FFN]:
        a = _np.ascontiguousarray(inputs[name])
        arrays[f"in_{name}_dram"] = a
        args.append(nc.dram_tensor(f"in_{name}_dram", a.shape, _mybir.dt.from_np(a.dtype), kind="ExternalInput").ap())
    shape = inputs["L0_attn_u"].shape
    out = nc.dram_tensor("out_0_dram", shape, _mybir.dt.float32, kind="ExternalOutput").ap()
    program(nc, *args, out)
    r = _run(nc, [arrays], core_ids=[0])
    return r.results[0]["out_0_dram"]
```

```python
import concourse.bass as bass
from concourse import mybir
from contextlib import ExitStack

F32 = mybir.dt.float32
F16 = mybir.dt.float16
BF16 = mybir.dt.bfloat16
I32 = mybir.dt.int32
AX_X = mybir.AxisListType.X
ALU = mybir.AluOpType
ACT = mybir.ActivationFunctionType

P = 128
BATCH, SEQ, DM = 2, 2048, 512
DI, NS, NH, HD, TAPS = 1024, 64, 16, 64, 4
DPROJ = 2 * DI + 2 * NS + NH
FF = 2048
TB = 256
NT = TB // P
NBLK = SEQ // TB
NBLOCKS = BATCH * NBLK
KD = DM // P
CX = DI // P
KF = FF // P
BC0 = 2 * DI
NBC = 2 * NS + NH
LN_EPS, RMS_EPS = 1e-5, 1e-6
LA_MIN = -1000.0
RSQRT_SEED = float(0x5F3759DF - (1 << 22) + (1 << 30))

PEAK = 2.0 ** 15
XN_SCALE = 2.0 ** 11
H_SCALE = PEAK / DM
Y_SCALE = PEAK / 1024
H_UNDO = 0.5 * H_SCALE / (PEAK * XN_SCALE) ** 2
WI_GROUPS = [((0, DI), 0), ((DI, DI), 2), ((BC0, 2 * NS), 4), ((BC0 + 2 * NS, NH), 5)]

TIMELINE = """
bc xp0 cv0 elu xp1 cv1 sv0 xp2 F0 sv1 F1
qk cs vt0 cv2 xp3 G vt1 dq00 dq01 sv2
F2 D0 dec00 cv3
F3 D1 dec01 vt2 sv3
F4 D2 vt3 vw00 dq02 dq03 int00
F5 D3 itr00 dec02
F6 D4 dec03 vw01 int01 st00
F7 D5 itr01 st01 ssq0 dq10 dq11
F8 D6 dec10 z00
F9 D7 z01 dec11 vw10
F10 D8 int10 yt00 yt01
F11 D9 ln itr10 O0 st10 dq12 dq13
F12 D10 dec12 dec13 vw11
int11 F13 itr11 D11 st11 ssq1
z10 F14 D12 z11
F15 D13 xt0 xt1 D14 yt10 yt11 D15 O1 fin
""".split()

PREPARATION = {-1: "sq0 ba0 bb0", 0: "nq0", 1: "nb0", 2: "nq1", 3: "nb1 nq2", 4: "nb2 nq3", 5: "nb3 nq4", 6: "nb4 nq5", 7: "nb5 ws",
               8: "dsq0 wi0", 9: "dsq1", 10: "dsq2 wi1", 11: "dsq3", 12: "wi2", 14: "wi3", 25: "dx2", 27: "dx3", 28: "pk",
               33: "wo0", 34: "wo1", 35: "wo2", 36: "wo3", 37: "wo4", 38: "wo5", 39: "wo6", 40: "wo7"}

RING_READER = {"bc": "dve", "xp": "act", "qk": "act", "cs": "act", "G": "dve", "vt": "act", "dec": "act",
               "int": "dve", "itr": "dve", "st": "dve", "z": "dve", "yt": "dve", "xt": "dve"}
BANKS = 4


def kind(step):
    return step.rstrip("0123456789")


def index(step):
    return [int(c) for c in step[len(kind(step)):]]


RING = [s for s in TIMELINE if kind(s) in RING_READER]
NR = len(RING)
NR_ACT = sum(RING_READER[kind(s)] == "act" for s in RING)
NR_DVE = NR - NR_ACT


def filled(step):
    return RING.index(step) + 1


def emptied(step):
    who = RING_READER[kind(step)]
    return sum(RING_READER[kind(s)] == who for s in RING[:RING.index(step) + 1])


def before(step):
    n = RING.index(step)
    if n >= BANKS:
        return RING[n - BANKS], 0
    return [s for m, s in enumerate(RING) if m % BANKS == n][-1], 1


def program(nc, u, in_w, conv_w, conv_b, a_log, dt_bias, d_param, norm_scale, out_w,
            su_ug, su_dp, ws_ug, ws_dp, w_up, w_gate, w_down, out):
    x_v = u.rearrange("b (n t p) d -> (b n) p t d", p=P, t=NT)
    out_v = out.rearrange("b (n t p) d -> (b n) p t d", p=P, t=NT)
    up_v = w_up.rearrange("(g t p) k -> g p t k", t=4, p=P)
    gate_v = w_gate.rearrange("(g t p) k -> g p t k", t=4, p=P)
    down_v = w_down.rearrange("(t p) k -> p t k", p=P)
    GR = FF // DM

    ctx = ExitStack()
    with ctx:
        def sem(name):
            return ctx.enter_context(nc.semaphore(name))

        def sb(name, shape, dt=F32):
            return ctx.enter_context(nc.sbuf_tensor(name, shape, dt))

        banks = [ctx.enter_context(nc.psum_tensor(f"bank{n}", [P, 512], F32)) for n in range(8)]

        wi = sb("wi", [P, KD, 2, DPROJ], F16)
        wug = sb("wug", [P, KD, 2, 2 * FF], F16)
        wd = sb("wd", [P, KF, 2, DM], F16)
        wo = sb("wo", [P, CX, 2, DM], F16)
        conv = sb("conv", [P, (TAPS + 1) * CX])
        row3 = sb("row3", [P, 3, NH])
        ident = sb("ident", [P, P])
        upto = sb("upto", [P, P])
        after = sb("after", [P, P])
        ones = sb("ones", [P, P])
        upto16 = sb("upto16", [P, P], F16)
        after16 = sb("after16", [P, P], F16)
        gate_scale = sb("gate_scale", [P, KF])
        scal = sb("scal", [P, 5])
        S_BC, S_DT, S_Z, S_Y, S_OUT = (scal[:, n:n + 1] for n in range(5))
        WS_UG, WS_DP, SU_UG, SU_DP, NORM, CONVW, CONVB = 0, 32, 36, 40, 56, 64, 96

        vec_loaded, bcast_loaded, wi_loaded, wo_loaded, wo_early = (sem(n) for n in ("vec_loaded", "bcast_loaded", "wi_loaded", "wo_loaded", "wo_early"))
        down_loaded = [sem("down_loaded0"), sem("down_loaded1")]
        consts_made, cols_filled, cols_ready = sem("consts_made"), sem("cols_filled"), sem("cols_ready")
        had_ready, negexp_ready = sem("had_ready"), sem("negexp_ready")
        nat_loaded, nat_squared, half_done, mixed_done, mixed_used = (sem(n) for n in ("nat_loaded", "nat_squared", "half_done", "mixed_done", "mixed_used"))
        wt_filled, wt_copied, hw_filled, hw_high, hw_stored = (sem(n) for n in ("wt_filled", "wt_copied", "hw_filled", "hw_high", "hw_stored"))
        piece_squared, piece_summed, norms_filled, norms_taken = (sem(n) for n in ("piece_squared", "piece_summed", "norms_filled", "norms_taken"))
        wi_scales, wi_high, wi_split, down_squared, down_scaled, down_mixed, down_rest = (sem(n) for n in ("wi_scales", "wi_high", "wi_split", "down_squared", "down_scaled", "down_mixed", "down_rest"))
        peaks_ready, peaks_turned, peaks_diag, peaks_filled, all_scales, wo_high, wo_split = (sem(n) for n in ("peaks_ready", "peaks_turned", "peaks_diag", "peaks_filled", "all_scales", "wo_high", "wo_split"))
        prepared = sem("prepared")

        with ExitStack() as prep:
            def tmp(name, shape, dt=F32):
                return prep.enter_context(nc.sbuf_tensor(name, shape, dt))

            big = tmp("big", [P, 4 * FF])
            down_nat = big[:, :].rearrange("p (t k) -> p t k", t=4)
            pair = tmp("pair", [P, 2, 4, DM])
            wo_nat = pair[:, :, :, :].rearrange("p s t n -> p (s t) n")
            wo32 = wo[:, :, :, :].rearrange("p a s n -> p (a s n)").bitcast(F32).rearrange("p (s t n) -> p s t n", s=2, t=4)
            nat, half = pair[:, 0, :, :], pair[:, 1, :, :]
            mixed = [wo32[:, n, :, :] for n in range(2)]
            down_mix = wd[:, :, :, :].rearrange("p a s n -> p (a s n)").bitcast(F32).rearrange("p (t k) -> p t k", t=4)
            zx_nat = [[wug[:, a, s, FF:2 * FF].bitcast(F32) for s in range(2)] for a in range(KD)]
            bc_nat = tmp("bc_nat", [P, KD, NBC])
            wi_flat = wi[:, :, :, :].rearrange("p a s n -> p (a s n)")
            wo_first = wi_flat[:, 0:2 * CX * DM].bitcast(F32).rearrange("p (a n) -> p a n", a=CX)
            square = [wi_flat[:, (2 * CX + n) * DM:(2 * CX + n + 1) * DM].bitcast(BF16) for n in range(8)]
            wt = [tmp(f"wt{n}", [P, 512]) for n in range(2)]
            hi0, hi1, hi2 = (wt[0][:, n * P:(n + 1) * P].bitcast(I32) for n in range(3))
            vec = tmp("vec", [104, P])
            brow = tmp("brow", [1, 3 * NH])
            had = tmp("had", [P, P])
            cols = tmp("cols", [P, 104])
            ones16 = tmp("ones16", [P, P], BF16)
            nsq = tmp("nsq", [P, 36])
            pw = tmp("pw", [P, 32])
            nat_scale = tmp("nat_scale", [P, 36])
            gu = tmp("gu", [P, KF])
            cmax = tmp("cmax", [P, 7])
            cpw = tmp("cpw", [P, 7])
            peak = tmp("peak", [P, 2])
            peak2 = tmp("peak2", [2, 3])
            glob = tmp("glob", [P, 16])
            down_store = tmp("down_store", [P, KF])
            wo_store = tmp("wo_store", [P, CX])

            UG_UNITS = 2 * GR * KD
            UNITS = UG_UNITS + KF

            def down_stage(stage):
                return (down_nat, down_mix) if stage % 2 == 0 else (down_mix, down_nat)

            def wi_src(a, col, w):
                if col >= BC0:
                    return bc_nat[:, a, col - BC0:col - BC0 + w]
                return zx_nat[a][col // DI][:, col % DI:col % DI + w]

            NORM_BLOCKS = [[(wo_first[:, a, :], cols[:, NORM + a:NORM + a + 1]) for a in range(CX)]]
            NORM_BLOCKS += [[(wi_src(a, c, w), 1.0) for a in range(KD)]
                            for c, w in [(c, 512) for c in range(0, BC0, 512)] + [(BC0, NBC)]]
            PIECE = [sum(len(b) for b in NORM_BLOCKS[:n]) for n in range(len(NORM_BLOCKS) + 1)]

            steps = {n: [] for n in range(-1, UNITS)}
            for n, what in PREPARATION.items():
                steps[n] += what.split()
            for g in range(1, 2 * GR):
                steps[max(4 * g - 6, -1)] += [f"sq{g}", f"ba{g}"]
                steps[max(4 * g - 5, 0)] += [f"bb{g}"]
            ORDER = steps[-1] + ["T0"]
            for n in range(UNITS):
                ORDER += ([f"T{n + 1}"] if n + 1 < UNITS else []) + [f"H{n}"] + steps[n]

            def parse(step):
                k = kind(step)
                return k, int(step[len(k):] or 0)

            block = ctx.enter_context(nc.Block())

            @block.sync
            def _(sp):
                def load_group(g):
                    sp.dma_start(nat, (up_v[g] if g < GR else gate_v[g - GR])).then_inc(nat_loaded, 16)

                for at, rows, src in ((WS_UG, 32, ws_ug), (WS_DP, 4, ws_dp), (SU_UG, 4, su_ug), (SU_DP, 16, su_dp), (NORM, 8, norm_scale), (CONVB, 8, conv_b)):
                    sp.dma_start(vec[at:at + rows, :], src.rearrange("(r p) -> r p", p=P)).then_inc(vec_loaded, 16)
                sp.dma_start(vec[CONVW:CONVW + 32, :], conv_w.rearrange("j (r p) -> (j r) p", p=P)).then_inc(vec_loaded, 16)
                for n, row in enumerate((dt_bias, a_log, d_param)):
                    sp.dma_start(brow[0:1, n * NH:(n + 1) * NH], row.rearrange("(a h) -> a h", a=1)).then_inc(bcast_loaded, 16)
                sp.dma_start(wo_first, out_w.rearrange("(a p) n -> p a n", p=P)).then_inc(wo_early, 16)
                for g in range(1, 2 * GR):
                    sp.wait_ge(nat_squared, g)
                    sp.wait_ge(half_done, g)
                    load_group(g)
                    if g == 1:
                        in_v = in_w.rearrange("(a p) n -> p a n", p=P)
                        for s in range(2):
                            sp.dma_start(wug[:, :, s, FF:2 * FF].bitcast(F32), in_v[:, :, s * DI:(s + 1) * DI]).then_inc(wi_loaded, 16)
                        sp.dma_start(bc_nat[:, :, :], in_v[:, :, BC0:DPROJ]).then_inc(wi_loaded, 16)
                    if g in (2, 3):
                        t = 2 * (g - 2)
                        sp.dma_start(down_nat[:, t:t + 2, :], down_v[:, t:t + 2, :]).then_inc(down_loaded[g - 2], 16)
                sp.wait_ge(nat_squared, 2 * GR)
                sp.wait_ge(mixed_done, 2 * GR)
                sp.dma_start(wo_nat, out_w.rearrange("(a p) n -> p a n", p=P)).then_inc(wo_loaded, 16)
                sp.sem_inc(prepared, 1)

            @block.gpsimd
            def _(pool):
                pool.memset(ones[:, :], 1.0)
                pool.memset(ones16[:, :], 1.0)
                pool.memset(ident[:, :], 0.0)
                pool.iota(hi0, [[0, P]], base=0, channel_multiplier=1)
                pool.iota(hi1, [[1, P]], base=0, channel_multiplier=0).then_inc(consts_made, 1)
                pool.wait_ge(consts_made, 1)
                pool.affine_select(out=ident[:, :], in_=ident[:, :], compare_op=ALU.not_equal, fill=1.0,
                                   base=0, pattern=[[-1, P]], channel_multiplier=1)
                pool.affine_select(out=upto[:, :], in_=ones[:, :], compare_op=ALU.is_ge, fill=0.0,
                                   base=0, pattern=[[1, P]], channel_multiplier=-1)
                pool.affine_select(out=after[:, :], in_=ones[:, :], compare_op=ALU.is_gt, fill=0.0,
                                   base=0, pattern=[[-1, P]], channel_multiplier=1).then_inc(consts_made, 1)
                pool.wait_ge(consts_made, 2)
                pool.tensor_copy(upto16[:, :], upto[:, :])
                pool.tensor_copy(after16[:, :], after[:, :]).then_inc(consts_made, 1)

                pool.wait_ge(cols_ready, 1)
                for t in range(KD):
                    pool.wait_ge(down_loaded[t // 2], 16)
                    pool.tensor_scalar(down_nat[:, t, :], down_nat[:, t, :], nat_scale[:, 32 + t:33 + t], None, ALU.mult).then_inc(down_scaled, 1)
                pool.wait_ge(down_scaled, KD)
                for stage in range(4):
                    if stage:
                        pool.wait_ge(down_mixed, stage)
                    if stage == 1:
                        pool.wait_ge(down_squared, KD)
                    a, b = down_stage(stage)
                    rows = slice(0, KD if stage < 2 else KD // 2)
                    va, vb = (x[:, rows, :].rearrange("p t (m c w) -> p (t m) c w", c=2, w=P << stage) for x in (a, b))
                    pool.tensor_tensor(vb[:, :, 0, :], va[:, :, 0, :], va[:, :, 1, :], ALU.add)
                    pool.tensor_tensor(vb[:, :, 1, :], va[:, :, 0, :], va[:, :, 1, :], ALU.subtract).then_inc(down_mixed, 1)
                pool.sem_inc(prepared, 1)

            @block.scalar
            def _(act):

                act.dma_start(nat, up_v[0]).then_inc(nat_loaded, 16)
                act.wait_ge(cols_filled, 1)
                nc.scalar.activation(cols[:, 0:104], banks[6][:, 0:104], ACT.Copy)
                nc.scalar.activation(row3[:, 0, :], banks[6][:, 128:128 + NH], ACT.Copy)
                nc.scalar.activation(row3[:, 1, :], banks[6][:, 128 + NH:128 + 2 * NH], ACT.Exp)
                nc.scalar.activation(row3[:, 2, :], banks[6][:, 128 + 2 * NH:128 + 3 * NH], ACT.Copy).then_inc(negexp_ready, 1)
                act.wait_ge(cols_ready, 1)
                for step in ORDER:
                    k, n = parse(step)
                    if k == "sq":
                        act.drain()
                        act.wait_ge(nat_loaded, 16 * (n + 1))
                        if n >= GR:
                            act.wait_ge(norms_taken, 6)
                        for t in range(4):
                            if n < GR:
                                dump = wug[:, t, 0, n * 512:(n + 1) * 512].bitcast(BF16)
                            else:
                                dump = banks[6 + t % 2][:, :]
                                if t == 2:
                                    act.drain()
                            ins = nc.scalar.activation(dump, nat[:, t, :], ACT.Square,
                                                       scale=cols[:, 4 * n + t:4 * n + t + 1], accum_out=nsq[:, 4 * n + t:4 * n + t + 1])
                        ins.then_inc(nat_squared, 1)
                    elif k == "nq":
                        if n == 0:
                            act.wait_ge(wo_early, 16)
                        if n == 1:
                            act.wait_ge(wi_loaded, 3 * 16)
                        for m, (src, scale) in enumerate(NORM_BLOCKS[n], PIECE[n]):
                            if m >= 8:
                                act.wait_ge(piece_summed, m - 7)
                            nc.scalar.activation(square[m % 8][:, 0:src.shape[-1]], src, ACT.Square, scale=scale).then_inc(piece_squared, 1)
                    elif k == "T":
                        act.wait_ge(wt_filled, n + 1)
                        if n >= 2:
                            act.wait_ge(hw_filled, n - 1)
                        nc.scalar.activation(wt[n % 2][:, :], banks[n % 2][:, :], ACT.Copy).then_inc(wt_copied, 1)
                    elif k == "H":
                        act.wait_ge(hw_filled, n + 1)
                        g, a = divmod(n, KD)
                        if n < UG_UNITS:
                            if n == GR * KD:
                                act.wait_ge(wi_split, 1)
                            dst, sc = wug[:, a, 0, g * 512:(g + 1) * 512], cols[:, SU_UG + a:SU_UG + a + 1]
                        else:
                            a = n - UG_UNITS
                            dst, sc = wd[:, a, 0, :], down_store[:, a:a + 1]
                        nc.scalar.activation(dst, banks[2 + n % 4][:, :], ACT.Copy, scale=sc).then_inc(hw_high, 1)
                    elif k == "wi":
                        act.drain()
                        act.wait_ge(wi_scales, 1)
                        for (c, w), s in WI_GROUPS:
                            ins = nc.scalar.activation(wi[:, n, 0, c:c + w], wi_src(n, c, w), ACT.Copy, scale=glob[:, s:s + 1])
                        ins.then_inc(wi_high, 1)
                    elif k == "dsq":
                        act.drain()
                        act.wait_ge(down_scaled, n + 1)
                        nc.scalar.activation(wi_flat[:, (KD - 1) * 2 * DPROJ:(KD - 1) * 2 * DPROJ + FF].bitcast(BF16), down_nat[:, n, :], ACT.Square,
                                             scale=float(FF) ** 0.5, accum_out=nsq[:, 32 + n:33 + n]).then_inc(down_squared, 1)
                    elif k == "pk":
                        act.wait_ge(all_scales, 1)
                    elif k == "wo":
                        act.wait_ge(wo_loaded, 16)
                        act.wait_ge(mixed_used, 2 * GR)
                        nc.scalar.activation(wo[:, n, 0, :], wo_nat[:, n, :], ACT.Copy, scale=wo_store[:, n:n + 1]).then_inc(wo_high, 1)
                act.drain().then_inc(prepared, 1)

            @block.vector
            def _(dve):
                dve.wait_ge(consts_made, 1)
                nc.vector.tensor_tensor(hi2, hi0, hi1, ALU.bitwise_and)
                dve.drain()
                for s in (4, 2, 1):
                    nc.vector.tensor_scalar(hi0, hi2, s, None, ALU.logical_shift_right)
                    dve.drain()
                    nc.vector.tensor_tensor(hi2, hi0, hi2, ALU.bitwise_xor)
                    dve.drain()
                nc.vector.tensor_scalar(hi0, hi2, 1, None, ALU.bitwise_and)
                dve.drain()
                nc.vector.tensor_scalar(had[:, :], hi0, -2.0, 1.0, ALU.mult, ALU.add).then_inc(had_ready, 1)

                def power_above(sq, out):
                    s, o = sq.bitcast(I32), out.bitcast(I32)
                    nc.vector.tensor_scalar(o, s, 23, None, ALU.logical_shift_right)
                    dve.drain()
                    nc.vector.tensor_scalar(o, o, 129.0, None, ALU.add)
                    dve.drain()
                    nc.vector.tensor_scalar(o, o, 1, 23, ALU.logical_shift_right, ALU.logical_shift_left)
                    dve.drain()

                def inverse_power(x, out):
                    nc.vector.tensor_scalar(out.bitcast(I32), x.bitcast(I32), -1.0, float(254 << 23), ALU.mult, ALU.add)
                    dve.drain()

                def butterfly(src, dst, w):
                    vs = src.rearrange("p t (m c w) -> p (t m) c w", c=2, w=w)
                    vd = dst.rearrange("p t (m c w) -> p (t m) c w", c=2, w=w)
                    nc.vector.tensor_tensor(vd[:, :, 0, :], vs[:, :, 0, :], vs[:, :, 1, :], ALU.add)
                    return nc.vector.tensor_tensor(vd[:, :, 1, :], vs[:, :, 0, :], vs[:, :, 1, :], ALU.subtract)

                def peaks():
                    dve.wait_ge(down_squared, 4)
                    nc.vector.tensor_tensor(gu[:, :], pw[:, 0:KF], pw[:, KF:2 * KF], ALU.mult)
                    dve.drain()
                    nc.vector.reduce_max(peak[:, 0:1], gu[:, :], AX_X)
                    nc.vector.reduce_max(peak[:, 1:2], nsq[:, 32:36], AX_X).then_inc(peaks_ready, 1)
                    nc.vector.tensor_scalar(gate_scale[:, :], pw[:, KF:2 * KF], 0.5 * undo, None, ALU.mult)
                    dve.wait_ge(peaks_turned, 1)
                    nc.vector.reduce_max(peak2[:, 0:1], banks[6][0:2, 0:P], AX_X)
                    dve.drain()
                    nc.vector.tensor_scalar(peak2[:, 1:3], ident[0:2, 0:2], peak2[:, 0:1], None, ALU.mult).then_inc(peaks_diag, 1)
                    dve.wait_ge(peaks_filled, 1)
                    nc.vector.tensor_copy(glob[:, 8:10], banks[7][:, 0:2])
                    dve.drain()
                    power_above(glob[:, 9:10], glob[:, 9:10])
                    power_above(cmax[:, 6:7], cpw[:, 6:7])
                    nc.vector.tensor_tensor(glob[:, 10:11], glob[:, 8:9], glob[:, 9:10], ALU.mult)
                    nc.vector.tensor_tensor(glob[:, 11:12], cpw[:, 0:1], cpw[:, 6:7], ALU.mult)
                    dve.drain()
                    nc.vector.tensor_scalar(glob[:, 10:11], glob[:, 10:11], 1.0 / (H_SCALE * PEAK), None, ALU.mult)
                    nc.vector.tensor_scalar(glob[:, 11:12], glob[:, 11:12], 1.0 / (Y_SCALE * PEAK), None, ALU.mult)
                    dve.drain()
                    nc.vector.tensor_tensor(S_OUT, glob[:, 10:11], glob[:, 11:12], ALU.max)
                    dve.drain()
                    inverse_power(S_OUT, glob[:, 12:13])
                    inverse_power(cpw[:, 0:1], glob[:, 13:14])
                    nc.vector.tensor_scalar(glob[:, 14:15], glob[:, 12:13], 1.0 / H_SCALE, None, ALU.mult)
                    nc.vector.scalar_tensor_tensor(glob[:, 15:16], cpw[:, 0:1], 1.0 / Y_SCALE, glob[:, 12:13], ALU.mult, ALU.mult)
                    nc.vector.scalar_tensor_tensor(S_Y, glob[:, 13:14], Y_SCALE, S_Z, ALU.mult, ALU.mult)
                    dve.drain()
                    nc.vector.scalar_tensor_tensor(down_store[:, :], gu[:, :], glob[:, 14:15], cols[:, SU_DP:SU_DP + KF], ALU.mult, ALU.mult)
                    nc.vector.tensor_scalar(wo_store[:, :], cols[:, NORM:NORM + CX], glob[:, 15:16], None, ALU.mult).then_inc(all_scales, 1)
                    dve.wait_ge(all_scales, 1)

                undo = 1.0 / (PEAK * XN_SCALE)
                for step in ORDER:
                    k, n = parse(step)
                    if k == "ba":
                        dve.wait_ge(nat_loaded, 16 * (n + 1))
                        butterfly(nat, half, P).then_inc(half_done, 1)
                        if n == 0:
                            dve.wait_ge(negexp_ready, 1)
                            nc.vector.tensor_scalar(row3[:, 1, :], row3[:, 1, :], -1.0, None, ALU.mult)
                            nc.vector.tensor_scalar(conv[:, :], cols[:, CONVW:CONVW + (TAPS + 1) * CX], 0.5, None, ALU.mult)
                            nc.vector.tensor_scalar(nat_scale[:, 32:36], cols[:, WS_DP:WS_DP + 4], float(FF) ** -0.5, None, ALU.mult).then_inc(cols_ready, 1)
                    elif k == "bb":
                        dve.wait_ge(nat_squared, n + 1)
                        c = slice(4 * n, 4 * n + 4)
                        power_above(nsq[:, c], pw[:, c])
                        if n >= 2:
                            dve.wait_ge(mixed_used, n - 1)
                        butterfly(half, mixed[n % 2], 2 * P)
                        inverse_power(pw[:, c], nat_scale[:, c])
                        nc.vector.scalar_tensor_tensor(nat_scale[:, c], nat_scale[:, c], PEAK * float(DM) ** -0.5, cols[:, c], ALU.mult, ALU.mult)
                        dve.drain()
                        for t in range(4):
                            ins = nc.vector.tensor_scalar(mixed[n % 2][:, t, :], mixed[n % 2][:, t, :], nat_scale[:, 4 * n + t:4 * n + t + 1], None, ALU.mult)
                        ins.then_inc(mixed_done, 1)
                    elif k == "H":
                        dve.wait_ge(hw_high, n + 1)
                        g, a = divmod(n, KD)
                        if n < UG_UNITS:
                            dst, sc = wug[:, a, :, g * 512:(g + 1) * 512], cols[:, SU_UG + a:SU_UG + a + 1]
                        else:
                            a = n - UG_UNITS
                            dst, sc = wd[:, a, :, :], down_store[:, a:a + 1]
                        nc.vector.scalar_tensor_tensor(dst[:, 1, :], banks[2 + n % 4][:, :], sc, dst[:, 0, :], ALU.mult, ALU.subtract).then_inc(hw_stored, 1)
                    elif k == "nb":
                        dve.wait_ge(norms_filled, n + 1)
                        o = banks[6 + n % 2]
                        if n == 5:
                            nc.vector.reduce_max(cmax[:, 4:5], o[:, 0:2 * NS], AX_X)
                            ins = nc.vector.reduce_max(cmax[:, 5:6], o[:, 2 * NS:NBC], AX_X)
                        else:
                            col = 6 if n == 0 else n - 1
                            ins = nc.vector.reduce_max(cmax[:, col:col + 1], o[:, :], AX_X)
                        ins.then_inc(norms_taken, 1)
                    elif k == "ws":
                        dve.drain()
                        nc.vector.tensor_tensor(cmax[:, 0:1], cmax[:, 0:1], cmax[:, 1:2], ALU.max)
                        nc.vector.tensor_tensor(cmax[:, 2:3], cmax[:, 2:3], cmax[:, 3:4], ALU.max)
                        dve.drain()
                        power_above(cmax[:, 0:6], cpw[:, 0:6])
                        inverse_power(cpw[:, 0:6], glob[:, 0:6])
                        nc.vector.tensor_scalar(glob[:, 0:6], glob[:, 0:6], PEAK, None, ALU.mult).then_inc(wi_scales, 1)
                        nc.vector.tensor_scalar(S_BC, cpw[:, 4:5], undo, None, ALU.mult)
                        nc.vector.tensor_scalar(S_DT, cpw[:, 5:6], undo, None, ALU.mult)
                        nc.vector.tensor_scalar(S_Z, cpw[:, 0:1], 0.5 * undo, None, ALU.mult)
                        nc.vector.tensor_scalar(glob[:, 6:7], cpw[:, 2:3], undo, None, ALU.mult)
                        dve.drain()
                        nc.vector.tensor_scalar(conv[:, 0:TAPS * CX], conv[:, 0:TAPS * CX], glob[:, 6:7], None, ALU.mult)
                    elif k == "wi":
                        dve.wait_ge(wi_high, n + 1)
                        for (c, w), s in WI_GROUPS:
                            ins = nc.vector.scalar_tensor_tensor(wi[:, n, 1, c:c + w], wi_src(n, c, w), glob[:, s:s + 1], wi[:, n, 0, c:c + w],
                                                                 ALU.mult, ALU.subtract)
                        if n == KD - 1:
                            ins.then_inc(wi_split, 1)
                            dve.wait_ge(wi_split, 1)
                    elif k == "dx":
                        dve.drain()
                        dve.wait_ge(down_mixed, 2)
                        a, b = down_stage(n)
                        butterfly(a[:, KD // 2:, :], b[:, KD // 2:, :], P << n).then_inc(down_rest, 1)
                    elif k == "pk":
                        peaks()
                    elif k == "wo":
                        dve.wait_ge(wo_high, n + 1)
                        nc.vector.scalar_tensor_tensor(wo[:, n, 1, :], wo_nat[:, n, :], wo_store[:, n:n + 1], wo[:, n, 0, :], ALU.mult, ALU.subtract).then_inc(wo_split, 1)
                dve.drain().then_inc(prepared, 1)

            @block.tensor
            def _(pe):
                pe.wait_ge(consts_made, 2)
                pe.wait_ge(vec_loaded, 7 * 16)
                nc.tensor.transpose(banks[6][:, 0:104], vec[:, :], ident[0:104, 0:104])
                pe.wait_ge(bcast_loaded, 3 * 16)
                nc.tensor.matmul(banks[6][:, 128:128 + 3 * NH], ones[0:1, :], brow[0:1, :], start=True, stop=True).then_inc(cols_filled, 1)
                pe.wait_ge(had_ready, 1)
                pe.wait_ge(negexp_ready, 1)
                for step in ORDER:
                    k, n = parse(step)
                    if k == "nb":
                        if n >= 2:
                            pe.wait_ge(norms_taken, n - 1)
                        for m, (src, _) in enumerate(NORM_BLOCKS[n], PIECE[n]):
                            pe.wait_ge(piece_squared, m + 1)
                            w = src.shape[-1]
                            nc.tensor.matmul(banks[6 + n % 2][:, 0:w], ones16[:, :], square[m % 8][:, 0:w],
                                             start=m == PIECE[n], stop=m == PIECE[n + 1] - 1).then_inc(piece_summed, 1)
                        pe.wait_ge(piece_summed, PIECE[n + 1])
                        pe.sem_inc(norms_filled, 1)
                    elif k == "T":
                        g, a = divmod(n, KD)
                        if n < UG_UNITS:
                            if a == 0:
                                pe.wait_ge(mixed_done, g + 1)
                            src = mixed[g % 2]
                        else:
                            a = n - UG_UNITS
                            pe.wait_ge(down_mixed, 4)
                            pe.wait_ge(down_rest, 2)
                            src = down_nat
                        if n >= 2:
                            pe.wait_ge(wt_copied, n - 1)
                        for t in range(4):
                            ins = nc.tensor.transpose(banks[n % 2][:, t * P:(t + 1) * P], src[:, t, a * P:(a + 1) * P], ident[:, :])
                        ins.then_inc(wt_filled, 1)
                        if n < UG_UNITS and a == KD - 1:
                            pe.wait_ge(wt_filled, n + 1)
                            pe.sem_inc(mixed_used, 1)
                    elif k == "H":
                        pe.wait_ge(wt_copied, n + 1)
                        if n >= 4:
                            pe.wait_ge(hw_stored, n - 3)
                        nc.tensor.matmul(banks[2 + n % 4][:, :], had[:, :], wt[n % 2][:, :], start=True, stop=True).then_inc(hw_filled, 1)
                    elif k == "pk":
                        pe.wait_ge(peaks_ready, 1)
                        pe.wait_ge(norms_taken, 6)
                        nc.tensor.transpose(banks[6][0:2, 0:P], peak[:, :], ident[:, :]).then_inc(peaks_turned, 1)
                        pe.wait_ge(peaks_diag, 1)
                        nc.tensor.matmul(banks[7][:, 0:2], ones[0:2, :], peak2[:, 1:3], start=True, stop=True).then_inc(peaks_filled, 1)
                pe.sem_inc(prepared, 1)

        v = sb("v", [P, NT, DI])
        dr = [sb(f"dr{n}", [P, 2, 4, P], F16) for n in range(2)]
        Mx = sb("Mx", [P, 2, 4, P])
        M = [Mx[:, n, :, :] for n in range(2)]
        res = Mx[:, :, :, :].rearrange("p a h s -> p a (h s)")
        yi = sb("yi", [P, 512])
        vw = [sb(f"vw{n}", [P, 512]) for n in range(2)]
        state = sb("state", [NS, DI])
        yT = sb("yT", [P, CX, 2, P], F16)
        h = [sb(f"h{n}", [P, 2, TB], F16) for n in range(3)]
        cvx = sb("cvx", [P, 2, 2, TB])
        stats = sb("stats", [P, NT, 6])
        mv = sb("mv", [P, NT, 2])
        rs = sb("rs", [P, 4, NT])
        xnT = sb("xnT", [P, KD, 2, TB], F16)
        xc = [sb(f"xc{n}", [P, 2, TAPS - 1 + TB]) for n in range(2)]
        halo = sb("halo", [P, CX, TAPS - 1])
        cv = [cvx[:, n, :, :] for n in range(2)]
        xin = cvx[:, :, :, :].rearrange("p a c t -> p a (c t)")
        ctz = sb("ctz", [P, 512])
        ct = ctz[:, :].rearrange("p (c t) -> p c t", c=2)
        zt = ctz
        junk = ctz[:, :].bitcast(F16)
        raw = sb("raw", [P, NT, NBC])
        neg = sb("neg", [P, NT, NBC])
        kq = sb("kq", [P, NT, 2 * NS])
        lns = sb("lns", [P, NT, NH])
        la = sb("la", [P, NT, NH])
        la16 = sb("la16", [P, 2, NT, NH], F16)
        qkT = sb("qkT", [NS, 2, NT, P])
        dec3 = sb("dec3", [P, 3, NT, NH])
        Gm = sb("Gm", [P, NT, P])
        vd = sb("vd", [P, 512])
        ssq = sb("ssq", [P, NT])
        tg = [sb(f"tg{n}", [P, TB]) for n in range(2)]

        ring = banks[0:BANKS]
        ug = banks[4:6]
        acc = banks[6:8]

        ring_filled, act_emptied, dve_emptied = sem("ring_filled"), sem("act_emptied"), sem("dve_emptied")
        ug_filled, h_ready, h_used = sem("ug_filled"), sem("h_ready"), sem("h_used")
        acc_filled, acc_emptied = sem("acc_filled"), sem("acc_emptied")
        tanh_gate, tanh_conv, tanh_z = sem("tanh_gate"), sem("tanh_conv"), sem("tanh_z")
        raw_ready, exps_done, ln_done, kq_ready = sem("raw_ready"), sem("exps_done"), sem("ln_done"), sem("kq_ready")
        conv_done, vT_ready, dr_ready, M_ready = sem("conv_done"), sem("vT_ready"), sem("dr_ready"), sem("M_ready")
        state_ready, vw_ready, y_ready, ssq_ready, yg_ready = (sem(n) for n in ("state_ready", "vw_ready", "y_ready", "ssq_ready", "yg_ready"))
        xn_ready, out_ready = sem("xn_ready"), sem("out_ready")
        h_whole, h_high, xn_high, y_high = sem("h_whole"), sem("h_high"), sem("xn_high"), sem("y_high")
        x_loaded, res_loaded, out_stored = sem("x_loaded"), sem("res_loaded"), sem("out_stored")

        def position(step):
            return ring[RING.index(step) % BANKS]

        def bcast(ap, n):
            return ap.unsqueeze(len(ap.shape)).to_broadcast(list(ap.shape) + [n])

        @block.sync
        def _(sp):
            sp.wait_ge(wo_split, CX)
            sp.dma_start(xin[:, :, :], x_v[0]).then_inc(x_loaded, 16)
            sp.wait_ge(prepared, 5)

            def step(i, following):
                sp.wait_ge(ring_filled, (i + 1) * NR + filled("vt3"))
                sp.dma_start(xin[:, :, :], x_v[following]).then_inc(x_loaded, 16)
                sp.wait_ge(ring_filled, (i + 1) * NR + filled("itr11"))
                sp.dma_start(res[:, :, :], x_v[i]).then_inc(res_loaded, 16)
                sp.wait_ge(out_ready, (i + 1) * NT)
                sp.dma_start(out_v[i], res[:, :, :]).then_inc(out_stored, 16)

            sp.sem_inc(out_stored, 16)
            with sp.Fori(0, NBLOCKS - 1) as i:
                step(i, i + 1)
            step(NBLOCKS - 1, 0)
            sp.wait_ge(x_loaded, 16 * (NBLOCKS + 1))
            sp.wait_ge(out_stored, 16 * (NBLOCKS + 1))

        @block.tensor
        def _(pe):
            pe.sem_inc(ring_filled, filled("xt0") - 1)
            for s, k in ((ug_filled, KF), (h_used, KF), (acc_filled, 1)):
                pe.sem_inc(s, k)
            pe.wait_ge(prepared, 5)

            def bank(i, s):
                prior, ago = before(s)
                reader, count = (act_emptied, NR_ACT) if RING_READER[kind(prior)] == "act" else (dve_emptied, NR_DVE)
                pe.wait_ge(reader, (i + 1 - ago) * count + emptied(prior))
                return position(s)

            def transpose_x(i, s):
                j, = index(s)
                pe.wait_ge(xn_ready, (i + 1) * NT + j + 1)
                o = bank(i, s)
                for a in range(KD):
                    ins = nc.tensor.transpose(o[:, a * P:(a + 1) * P], xin[:, j, a * P:(a + 1) * P], ident[:, :])
                ins.then_inc(ring_filled, 1)

            def products(out, pairs, first=True, last=True):
                for n, (lhsT, rhs) in enumerate(pairs):
                    ins = nc.tensor.matmul(out, lhsT, rhs, start=first and n == 0, stop=last and n == len(pairs) - 1)
                return ins

            def three(lhsT, rhs):
                return [(lhsT(0), rhs(0)), (lhsT(0), rhs(1)), (lhsT(1), rhs(0))]

            def body(i):
                for s in TIMELINE:
                    k, at = kind(s), index(s)
                    if k == "bc":
                        pe.wait_ge(dve_emptied, i * NR_DVE + emptied("xt1"))
                        o = bank(i, s)
                        for j in range(NT):
                            ins = products(o[:, j * NBC:(j + 1) * NBC],
                                           [pq for a in range(KD) for pq in three(lambda u: xnT[:, a, u, j * P:(j + 1) * P], lambda u: wi[:, a, u, BC0:DPROJ])])
                        ins.then_inc(ring_filled, 1)
                    elif k == "xp":
                        o = bank(i, s)
                        for c in range(2):
                            col = DI + (2 * at[0] + c) * P
                            ins = products(o[:, c * TB:(c + 1) * TB],
                                           [pq for a in range(KD) for pq in three(lambda u: wi[:, a, u, col:col + P], lambda u: xnT[:, a, u, :])])
                        ins.then_inc(ring_filled, 1)
                    elif k == "F":
                        c = at[0] if len(at) == 1 else 10 * at[0] + at[1]
                        pe.wait_ge(h_ready, (i + 1) * KF + c - 1)
                        for n, col in enumerate((FF + c * P, c * P)):
                            ins = products(ug[c % 2][:, n * TB:(n + 1) * TB],
                                           [pq for a in range(KD) for pq in three(lambda u: wug[:, a, u, col:col + P], lambda u: xnT[:, a, u, :])])
                        ins.then_inc(ug_filled, 1)
                    elif k == "D":
                        c = at[0] if len(at) == 1 else 10 * at[0] + at[1]
                        if c == 0:
                            pe.wait_ge(acc_emptied, i + 1)
                        pe.wait_ge(h_ready, (i + 1) * KF + c + 1)
                        for j in range(NT):
                            ins = products(acc[j][:, :], three(lambda u: h[c % 3][:, u, j * P:(j + 1) * P], lambda u: wd[:, c, u, :]),
                                           first=c == 0, last=c == KF - 1 and j == 0)
                        ins.then_inc(h_used, 1)
                    elif k == "qk":
                        pe.wait_ge(kq_ready, i + 2)
                        o = bank(i, s)
                        for n in range(2):
                            for j in range(NT):
                                ins = products(o[0:NS, (n * NT + j) * P:(n * NT + j + 1) * P],
                                               [(kq[:, j, n * NS:(n + 1) * NS], ident[:, :])])
                        ins.then_inc(ring_filled, 1)
                    elif k == "cs":
                        o = bank(i, s)
                        for n, w in enumerate((upto, after, ones)):
                            ins = products(o[:, n * NT * NH:(n + 1) * NT * NH],
                                           [(w[:, :], la[:, :, :].rearrange("p t h -> p (t h)"))])
                        ins.then_inc(ring_filled, 1)
                    elif k == "G":
                        pe.wait_ge(act_emptied, (i + 1) * NR_ACT + emptied("qk"))
                        o = bank(i, s)
                        for j in range(NT):
                            ins = products(o[:, j * P:(j + 1) * P], [(qkT[:, 0, j, :], qkT[:, 1, j, :])])
                        ins.then_inc(ring_filled, 1)
                    elif k == "vt":
                        pe.wait_ge(vT_ready, (i + 1) * 4 + at[0] + 1)
                        o = bank(i, s)
                        for j in range(NT):
                            for c in range(2):
                                ins = nc.tensor.transpose(o[:, (2 * j + c) * P:(2 * j + c + 1) * P],
                                                          cv[at[0] % 2][:, c, j * P:(j + 1) * P], ident[:, :])
                        ins.then_inc(ring_filled, 1)
                    elif k == "dec":
                        c, q = at
                        pe.wait_ge(dr_ready, (i + 1) * 8 + 4 * c + q + 1)
                        o = bank(i, s)
                        products(o[:, :], [(after16[:, :], dr[q % 2][:, n, :, :].rearrange("p h s -> p (h s)"))
                                           for n in range(2)]).then_inc(ring_filled, 1)
                    elif k == "int":
                        c, hf = at
                        pe.wait_ge(state_ready, (i + 1) * 4 + 2 * c + hf - 1)
                        o = bank(i, s)
                        products(o[:, :], [(qkT[:, 1, c, :], state[:, hf * 512:(hf + 1) * 512])]).then_inc(ring_filled, 1)
                    elif k == "itr":
                        c, hf = at
                        pe.wait_ge(M_ready, (i + 1) * 8 + 4 * c + 2 * hf + 2)
                        pe.wait_ge(act_emptied, (i + 1) * NR_ACT + emptied("vt3"))
                        o = bank(i, s)
                        for n in range(8):
                            hd = 8 * hf + n
                            ins = products(o[:, n * HD:(n + 1) * HD],
                                           [(M[n // 4][:, n % 4, :], v[:, c, hd * HD:(hd + 1) * HD])])
                        ins.then_inc(ring_filled, 1)
                    elif k == "st":
                        c, hf = at
                        pe.wait_ge(vw_ready, (i + 1) * 4 + 2 * c + hf + 1)
                        o = bank(i, s)
                        products(o[0:NS, :], [(kq[:, c, 0:NS], vw[hf][:, :])]).then_inc(ring_filled, 1)
                    elif k == "z":
                        c, hf = at
                        o = bank(i, s)
                        products(o[:, :], [pq for a in range(KD) for pq in three(lambda u: xnT[:, a, u, c * P:(c + 1) * P],
                                                                                  lambda u: wi[:, a, u, hf * 512:(hf + 1) * 512])]).then_inc(ring_filled, 1)
                    elif k == "yt":
                        c, hf = at
                        pe.wait_ge(yg_ready, (i + 1) * 4 + 2 * c + hf + 1)
                        o = bank(i, s)
                        for n in range(4):
                            ins = nc.tensor.transpose(o[:, n * P:(n + 1) * P], v[:, c, (4 * hf + n) * P:(4 * hf + n + 1) * P], ident[:, :])
                        ins.then_inc(ring_filled, 1)
                    elif k == "O":
                        c = at[0]
                        pe.wait_ge(dve_emptied, (i + 1) * NR_DVE + emptied(f"yt{c}1"))
                        ins = products(acc[c][:, :], [pq for a in range(CX) for pq in three(lambda u: yT[:, a, u, :], lambda u: wo[:, a, u, :])],
                                       first=False, last=c == NT - 1)
                        if c == NT - 1:
                            ins.then_inc(acc_filled, 1)
                    elif k == "xt":
                        transpose_x(i, s)

            transpose_x(-1, "xt0")
            transpose_x(-1, "xt1")
            pe.wait_ge(ring_filled, filled("xt1"))
            pe.sem_inc(ring_filled, NR - filled("xt1"))
            with pe.Fori(0, NBLOCKS) as i:
                body(i)

        @block.scalar
        def _(act):
            act.sem_inc(act_emptied, NR_ACT)
            for s, k in ((h_high, KF), (y_high, 4), (tanh_gate, KF), (tanh_conv, 4), (tanh_z, 4), (exps_done, 1), (ln_done, 1), (ssq_ready, NT)):
                act.sem_inc(s, k)
            act.wait_ge(prepared, 5)

            def copy_xn(i, s):
                j, = index(s)
                act.wait_ge(ring_filled, (i + 1) * NR + filled(s))
                nc.scalar.activation(xnT[:, :, 0, j * P:(j + 1) * P], position(s)[:, :].rearrange("p (a t) -> p a t", a=KD),
                                     ACT.Copy, scale=XN_SCALE).then_inc(xn_high, 1)

            def body(i):
                def ring_has(s):
                    act.wait_ge(ring_filled, (i + 1) * NR + filled(s))
                    return position(s)

                for s in TIMELINE:
                    k, at = kind(s), index(s)
                    if k == "xp":
                        o = ring_has(s)
                        act.wait_ge(conv_done, (i + 1) * 4 + at[0] - 1)
                        nc.scalar.activation(xc[at[0] % 2][:, :, TAPS - 1:],
                                             o[:, :].rearrange("p (c t) -> p c t", c=2), ACT.Copy).then_inc(act_emptied, 1)
                    elif k == "elu":
                        act.wait_ge(raw_ready, i + 2)
                        nc.scalar.activation(neg[:, :, :], neg[:, :, :], ACT.Exp).then_inc(exps_done, 1)
                        act.drain()
                        nc.scalar.activation(lns[:, :, :], neg[:, :, 2 * NS:], ACT.Ln, bias=1.0).then_inc(ln_done, 1)
                    elif k == "sv":
                        act.wait_ge(conv_done, (i + 1) * 4 + at[0] + 1)
                        act.wait_ge(vT_ready, (i + 1) * 4 + at[0])
                        act.wait_ge(yg_ready, (i + 1) * 4)
                        nc.scalar.activation(ct[:, :, :], cv[at[0] % 2][:, :, :], ACT.Tanh).then_inc(tanh_conv, 1)
                    elif k == "F":
                        c = at[0] if len(at) == 1 else 10 * at[0] + at[1]
                        act.wait_ge(ug_filled, (i + 1) * KF + c + 1)
                        act.wait_ge(h_ready, (i + 1) * KF + c - 1)
                        nc.scalar.activation(tg[c % 2][:, :], ug[c % 2][:, 0:TB], ACT.Tanh,
                                             scale=gate_scale[:, c:c + 1]).then_inc(tanh_gate, 1)
                        act.wait_ge(h_used, (i + 1) * KF + c - 2)
                        act.wait_ge(h_whole, (i + 1) * KF + c + 1)
                        nc.scalar.activation(h[c % 3][:, 0, :], tg[c % 2][:, :], ACT.Copy).then_inc(h_high, 1)
                    elif k == "qk":
                        o = ring_has(s)
                        nc.scalar.activation(qkT[:, :, :, :].rearrange("n a t p -> n (a t p)"), o[0:NS, :], ACT.Copy).then_inc(act_emptied, 1)
                    elif k == "cs":
                        o = ring_has(s)
                        act.wait_ge(dve_emptied, i * NR_DVE + emptied("st11"))
                        act.wait_ge(vw_ready, (i + 1) * 4)
                        nc.scalar.activation(dec3[:, :, :, :].rearrange("p a t h -> p (a t h)"), o[:, 0:3 * NT * NH], ACT.Exp).then_inc(act_emptied, 1)
                    elif k == "vt":
                        o = ring_has(s)
                        nc.scalar.activation(v[:, :, 2 * at[0] * P:(2 * at[0] + 2) * P],
                                             o[:, :].rearrange("p (t c) -> p t c", t=NT), ACT.Copy).then_inc(act_emptied, 1)
                    elif k == "dec":
                        c, q = at
                        o = ring_has(s)
                        if c == 0 and q < 2:
                            act.wait_ge(out_stored, (i + 1) * 16)
                        else:
                            act.wait_ge(ring_filled, (i + 1) * NR + filled(f"itr{(4 * c + q - 2) // 4}{(4 * c + q - 2) % 4 // 2}"))
                        nc.scalar.activation(M[q % 2][:, :, :].rearrange("p h s -> p (h s)"), o[:, :], ACT.Exp).then_inc(act_emptied, 1)
                    elif k == "ssq":
                        act.drain()
                        act.wait_ge(y_ready, (i + 1) * 4 + 2 * at[0] + 2)
                        act.wait_ge(yg_ready, (i + 1) * 4 + 2 * at[0])
                        nc.scalar.activation(junk[:, :], v[:, at[0], :], ACT.Square, accum_out=ssq[:, at[0]:at[0] + 1]).then_inc(ssq_ready, 1)
                    elif k == "z":
                        act.drain()
                        o = ring_has(s)
                        act.wait_ge(yg_ready, (i + 1) * 4 + 2 * at[0] + at[1])
                        nc.scalar.activation(zt[:, :], o[:, :], ACT.Tanh, scale=S_Z).then_inc(tanh_z, 1)
                    elif k == "yt":
                        o = ring_has(s)
                        nc.scalar.activation(yT[:, 4 * at[1]:4 * at[1] + 4, 0, :],
                                             o[:, :].rearrange("p (a t) -> p a t", a=4), ACT.Copy).then_inc(y_high, 1)
                    elif k == "xt":
                        copy_xn(i, s)

            copy_xn(-1, "xt0")
            copy_xn(-1, "xt1")
            with act.Fori(0, NBLOCKS) as i:
                body(i)

        @block.gpsimd
        def _(pool):
            for s, k in ((dr_ready, 8), (vw_ready, 4)):
                pool.sem_inc(s, k)
            pool.wait_ge(prepared, 5)
            with pool.Fori(0, NBLOCKS) as i:
                for s in TIMELINE:
                    k, at = kind(s), index(s)
                    if k == "dq":
                        c, q = at
                        if c == 0 and q == 0:
                            pool.wait_ge(kq_ready, i + 2)
                        if c == 0 and q < 2:
                            pool.wait_ge(ring_filled, i * NR + filled(f"dec1{q + 2}"))
                        else:
                            pool.wait_ge(ring_filled, (i + 1) * NR + filled(f"dec{(4 * c + q - 2) // 4}{(4 * c + q - 2) % 4}"))
                        pool.tensor_tensor(dr[q % 2][:, :, :, :], bcast(la16[:, :, c, 4 * q:4 * q + 4], P),
                                           upto16[:, :].unsqueeze(1).unsqueeze(1).to_broadcast([P, 2, 4, P]),
                                           ALU.mult).then_inc(dr_ready, 1)
                    elif k == "vw":
                        c, hf = at
                        pool.wait_ge(act_emptied, (i + 1) * NR_ACT + emptied("vt3"))
                        if c == 0:
                            pool.wait_ge(ring_filled, i * NR + filled(f"st1{hf}"))
                        else:
                            pool.wait_ge(ring_filled, (i + 1) * NR + filled(f"st0{hf}"))
                        n = 2 * c + hf
                        if n == 0:
                            pool.wait_ge(dve_emptied, i * NR_DVE + emptied("int11"))
                        else:
                            pool.wait_ge(dve_emptied, (i + 1) * NR_DVE + emptied(f"int{(n - 1) // 2}{(n - 1) % 2}"))
                        vh = v[:, c, hf * 512:(hf + 1) * 512].rearrange("p (h d) -> p h d", d=HD)
                        pool.tensor_tensor(vw[hf][:, :].rearrange("p (h d) -> p h d", d=HD), vh,
                                           bcast(dec3[:, 1, c, 8 * hf:8 * hf + 8], HD), ALU.mult)
                        pool.tensor_tensor(vd[:, :].rearrange("p (h d) -> p h d", d=HD), vh,
                                           bcast(row3[:, 2, 8 * hf:8 * hf + 8], HD), ALU.mult).then_inc(vw_ready, 1)

        @block.vector
        def _(dve):
            dve.sem_inc(dve_emptied, emptied("xt0") - 1)
            for s, k in ((h_whole, KF), (h_ready, KF), (acc_emptied, 1), (raw_ready, 1), (kq_ready, 1), (conv_done, 4),
                         (vT_ready, 4), (M_ready, 8), (state_ready, 4), (y_ready, 4), (yg_ready, 4)):
                dve.sem_inc(s, k)

            def rsqrt(xh, y, a):
                nc.vector.tensor_scalar(a.bitcast(I32), xh.bitcast(I32), 1, None, ALU.logical_shift_right)
                dve.drain()
                nc.vector.tensor_scalar(y.bitcast(I32), a.bitcast(I32), -1.0, RSQRT_SEED, ALU.mult, ALU.add)
                dve.drain()
                for _ in range(3):
                    for j in range(xh.shape[-1]):
                        c = slice(j, j + 1)
                        nc.vector.tensor_scalar(a[:, c], y[:, c], y[:, c], xh[:, c], ALU.mult, ALU.mult)
                    dve.drain()
                    nc.vector.scalar_tensor_tensor(y, a, 1.5, y, ALU.add, ALU.mult)
                    dve.drain()

            def layer_norm(i):
                dve.wait_ge(x_loaded, (i + 2) * 16)
                for j in range(NT):
                    nc.vector.bn_stats(stats[:, j, :], xin[:, j, :])
                dve.drain()
                for j in range(NT):
                    nc.vector.bn_aggr(mv[:, j, :], stats[:, j, :])
                dve.drain()
                nc.vector.tensor_scalar(rs[:, 0, :], mv[:, :, 1], -0.5, -0.5 * LN_EPS, ALU.mult, ALU.add)
                dve.drain()
                rsqrt(rs[:, 0, :], rs[:, 1, :], rs[:, 2, :])
                for j in range(NT):
                    nc.vector.tensor_scalar(xin[:, j, :], xin[:, j, :], mv[:, j, 0:1], rs[:, 1, j:j + 1],
                                            ALU.subtract, ALU.mult).then_inc(xn_ready, 1)

            def body(i):
                def ring_has(s):
                    dve.wait_ge(ring_filled, (i + 1) * NR + filled(s))
                    return position(s)

                for s in TIMELINE:
                    k, at = kind(s), index(s)
                    if k == "bc":
                        o = ring_has(s)
                        o = o[:, 0:NT * NBC].rearrange("p (t n) -> p t n", t=NT)
                        nc.vector.tensor_scalar(raw[:, :, 0:2 * NS], o[:, :, 0:2 * NS], S_BC, None, ALU.mult)
                        nc.vector.scalar_tensor_tensor(raw[:, :, 2 * NS:], o[:, :, 2 * NS:], S_DT,
                                                       row3[:, 0, :].unsqueeze(1).to_broadcast([P, NT, NH]), ALU.mult, ALU.add).then_inc(dve_emptied, 1)
                        dve.drain()
                        nc.vector.tensor_scalar(neg[:, :, 0:2 * NS], raw[:, :, 0:2 * NS], 0.0, None, ALU.min)
                        dve.drain()
                        nc.vector.scalar_tensor_tensor(neg[:, :, 2 * NS:], raw[:, :, 2 * NS:], -1.0, raw[:, :, 2 * NS:], ALU.mult, ALU.min).then_inc(raw_ready, 1)
                    elif k == "elu":
                        dve.wait_ge(exps_done, i + 2)
                        nc.vector.scalar_tensor_tensor(kq[:, :, :], raw[:, :, 0:2 * NS], 0.0, neg[:, :, 0:2 * NS], ALU.max, ALU.add)
                        dve.wait_ge(ln_done, i + 2)
                        nc.vector.scalar_tensor_tensor(lns[:, :, :], raw[:, :, 2 * NS:], 0.0, lns[:, :, :], ALU.max, ALU.add)
                        dve.drain()
                        nc.vector.tensor_tensor(la[:, :, :], lns[:, :, :], row3[:, 1, :].unsqueeze(1).to_broadcast([P, NT, NH]), ALU.mult)
                        dve.drain()
                        nc.vector.tensor_scalar(la[:, :, :], la[:, :, :], LA_MIN, None, ALU.max)
                        dve.drain()
                        nc.vector.tensor_copy(la16[:, 0, :, :], la[:, :, :])
                        dve.drain()
                        nc.vector.tensor_tensor(la16[:, 1, :, :], la[:, :, :], la16[:, 0, :, :], ALU.subtract).then_inc(kq_ready, 1)
                    elif k == "cv":
                        n = at[0]
                        dve.wait_ge(act_emptied, (i + 1) * NR_ACT + emptied(f"xp{n}"))
                        dve.wait_ge(ring_filled, (i + 1) * NR + (0 if n < 2 else filled(f"vt{n - 2}")))
                        x = xc[n % 2]
                        nc.vector.tensor_copy(x[:, :, 0:TAPS - 1], halo[:, 2 * n:2 * n + 2, :])
                        for c in range(2):
                            t = 2 * n + c
                            nc.vector.tensor_scalar(cv[n % 2][:, c, :], x[:, c, 3:3 + TB], conv[:, 3 * CX + t:3 * CX + t + 1],
                                                    conv[:, TAPS * CX + t:TAPS * CX + t + 1], ALU.mult, ALU.add)
                        for j in range(3):
                            dve.drain()
                            for c in range(2):
                                t = 2 * n + c
                                ins = nc.vector.scalar_tensor_tensor(cv[n % 2][:, c, :], x[:, c, j:j + TB],
                                                                     conv[:, CX * j + t:CX * j + t + 1],
                                                                     cv[n % 2][:, c, :], ALU.mult, ALU.add)
                        nc.vector.tensor_copy(halo[:, 2 * n:2 * n + 2, :], x[:, :, TB:TB + TAPS - 1]).then_inc(conv_done, 1)
                    elif k == "sv":
                        n = at[0]
                        dve.wait_ge(tanh_conv, (i + 1) * 4 + n + 1)
                        nc.vector.scalar_tensor_tensor(cv[n % 2][:, :, :], ct[:, :, :], 1.0, cv[n % 2][:, :, :], ALU.add, ALU.mult).then_inc(vT_ready, 1)
                    elif k == "F":
                        c = at[0] if len(at) == 1 else 10 * at[0] + at[1]
                        dve.wait_ge(tanh_gate, (i + 1) * KF + c + 1)
                        nc.vector.scalar_tensor_tensor(tg[c % 2][:, :], tg[c % 2][:, :], 1.0, ug[c % 2][:, 0:TB], ALU.add, ALU.mult)
                        dve.drain()
                        nc.vector.scalar_tensor_tensor(tg[c % 2][:, :], tg[c % 2][:, :], H_UNDO, ug[c % 2][:, TB:2 * TB], ALU.mult, ALU.mult).then_inc(h_whole, 1)
                        dve.wait_ge(h_high, (i + 1) * KF + c + 1)
                        nc.vector.tensor_tensor(h[c % 3][:, 1, :], tg[c % 2][:, :], h[c % 3][:, 0, :], ALU.subtract).then_inc(h_ready, 1)
                    elif k == "G":
                        o = ring_has(s)
                        nc.vector.tensor_tensor(Gm[:, :, :], o[:, 0:NT * P].rearrange("p (t s) -> p t s", t=NT),
                                                upto[:, :].unsqueeze(1).to_broadcast([P, NT, P]), ALU.mult).then_inc(dve_emptied, 1)
                    elif k == "dec":
                        c, q = at
                        dve.drain()
                        dve.wait_ge(act_emptied, (i + 1) * NR_ACT + emptied(s))
                        nc.vector.tensor_tensor(M[q % 2][:, :, :], M[q % 2][:, :, :],
                                                Gm[:, c, :].unsqueeze(1).to_broadcast([P, 4, P]), ALU.mult).then_inc(M_ready, 1)
                    elif k == "int":
                        c, hf = at
                        o = ring_has(s)
                        nc.vector.tensor_tensor(yi[:, :].rearrange("p (h d) -> p h d", d=HD), o[:, :].rearrange("p (h d) -> p h d", d=HD),
                                                bcast(dec3[:, 0, c, 8 * hf:8 * hf + 8], HD), ALU.mult)
                        dve.drain()
                        dve.wait_ge(vw_ready, (i + 1) * 4 + 2 * c + hf + 1)
                        nc.vector.tensor_tensor(yi[:, :], yi[:, :], vd[:, :], ALU.add).then_inc(dve_emptied, 1)
                    elif k == "itr":
                        c, hf = at
                        dve.drain()
                        o = ring_has(s)
                        ins = nc.vector.tensor_tensor(v[:, c, hf * 512:(hf + 1) * 512], o[:, :], yi[:, :], ALU.add)
                        ins.then_inc(y_ready, 1)
                        dve.wait_ge(y_ready, (i + 1) * 4 + 2 * c + hf + 1)
                        dve.sem_inc(dve_emptied, 1)
                    elif k == "st":
                        c, hf = at
                        half = state[:, hf * 512:(hf + 1) * 512]
                        o = ring_has(s)
                        nc.vector.tensor_tensor(half.rearrange("p (h d) -> p h d", d=HD), half.rearrange("p (h d) -> p h d", d=HD),
                                                bcast(dec3[0:NS, 2, c, 8 * hf:8 * hf + 8], HD), ALU.mult)
                        dve.drain()
                        nc.vector.tensor_tensor(half, o[0:NS, :], half, ALU.add).then_inc(state_ready, 1)
                        dve.wait_ge(state_ready, (i + 1) * 4 + 2 * c + hf + 1)
                        dve.sem_inc(dve_emptied, 1)
                    elif k == "ssq":
                        dve.wait_ge(ssq_ready, (i + 1) * NT + at[0] + 1)
                        c = slice(at[0], at[0] + 1)
                        nc.vector.tensor_scalar(rs[:, 0, c], ssq[:, c], -0.5 / DI, -0.5 * RMS_EPS, ALU.mult, ALU.add)
                        dve.drain()
                        rsqrt(rs[:, 0, c], rs[:, 3, c], rs[:, 2, c])
                        nc.vector.tensor_scalar(rs[:, 3, c], rs[:, 3, c], S_Y, None, ALU.mult)
                        dve.drain()
                    elif k == "z":
                        c, hf = at
                        dve.wait_ge(tanh_z, (i + 1) * 4 + 2 * c + hf + 1)
                        nc.vector.scalar_tensor_tensor(zt[:, :], zt[:, :], 1.0, position(s)[:, :], ALU.add, ALU.mult).then_inc(dve_emptied, 1)
                        dve.drain()
                        vh = v[:, c, hf * 512:(hf + 1) * 512]
                        nc.vector.scalar_tensor_tensor(vh, vh, rs[:, 3, c:c + 1], zt[:, :], ALU.mult, ALU.mult).then_inc(yg_ready, 1)
                    elif k == "yt":
                        dve.wait_ge(y_high, (i + 1) * 4 + 2 * at[0] + at[1] + 1)
                        part = yT[:, 4 * at[1]:4 * at[1] + 4, :, :]
                        nc.vector.tensor_tensor(part[:, :, 1, :], position(s)[:, :].rearrange("p (a t) -> p a t", a=4),
                                                part[:, :, 0, :], ALU.subtract).then_inc(dve_emptied, 1)
                    elif k == "xt":
                        low_xn(i, s)
                    elif k == "ln":
                        layer_norm(i)
                    elif k == "fin":
                        dve.wait_ge(res_loaded, (i + 1) * 16)
                        dve.wait_ge(acc_filled, i + 2)
                        for j in range(NT):
                            nc.vector.scalar_tensor_tensor(res[:, j, :], acc[j][:, :], S_OUT, res[:, j, :], ALU.mult, ALU.add).then_inc(out_ready, 1)
                        dve.wait_ge(out_ready, (i + 1) * NT)
                        dve.sem_inc(acc_emptied, 1)

            def low_xn(i, s):
                j, = index(s)
                dve.wait_ge(xn_high, (i + 1) * NT + j + 1)
                part = xnT[:, :, :, j * P:(j + 1) * P]
                nc.vector.scalar_tensor_tensor(part[:, :, 1, :], position(s)[:, :].rearrange("p (a t) -> p a t", a=KD), XN_SCALE,
                                               part[:, :, 0, :], ALU.mult, ALU.subtract).then_inc(dve_emptied, 1)

            layer_norm(-1)
            dve.wait_ge(prepared, 5)
            low_xn(-1, "xt0")
            low_xn(-1, "xt1")
            dve.wait_ge(dve_emptied, emptied("xt1"))
            dve.sem_inc(dve_emptied, NR_DVE - emptied("xt1"))
            with dve.Fori(0, BATCH) as b:
                nc.vector.memset(state[:, :], 0.0)
                nc.vector.memset(halo[:, :, :], 0.0)
                dve.drain()
                with dve.Fori(0, NBLK) as j:
                    body(b * NBLK + j)


_INS = ["u", "in_proj_w", "conv_weight", "conv_bias", "A_log", "dt_bias", "D_param", "norm_scale", "out_proj_w"]
_FFN = ["SU_ug", "SU_dp", "Wscale_ug", "Wscale_dp", "W_up", "W_gate", "W_down"]


def kernel(**inputs):
    import numpy as _np
    import concourse.bacc as _bacc
    from concourse import mybir as _mybir
    from concourse.bass_utils import run_bass_kernel_spmd as _run

    nc = _bacc.Bacc("TRN2", target_bir_lowering=False, num_devices=1)
    arrays, args = {}, []
    for name in [f"L0_attn_{n}" for n in _INS] + [f"L0_ffn_{n}" for n in _FFN]:
        a = _np.ascontiguousarray(inputs[name])
        arrays[f"in_{name}_dram"] = a
        args.append(nc.dram_tensor(f"in_{name}_dram", a.shape, _mybir.dt.from_np(a.dtype), kind="ExternalInput").ap())
    shape = inputs["L0_attn_u"].shape
    out = nc.dram_tensor("out_0_dram", shape, _mybir.dt.float32, kind="ExternalOutput").ap()
    program(nc, *args, out)
    r = _run(nc, [arrays], core_ids=[0])
    return r.results[0]["out_0_dram"]
```
